# Optimizing a Trainium2 kernel written in Bass

```python
import numpy as np
import jax
import jax.numpy as jnp

def _softmax(x, axis=-1):
    return jax.nn.softmax(x, axis=axis)

def _gelu(x):
    return jax.nn.gelu(x, approximate=True)

def _silu(x):
    return jax.nn.silu(x)

def _sigmoid(x):
    return jax.nn.sigmoid(x)

def _layernorm(x, axis=-1, eps=1e-05):
    m = jnp.mean(x, axis=axis, keepdims=True)
    v = jnp.var(x, axis=axis, keepdims=True)
    return (x - m) / jnp.sqrt(v + eps)

def _scatter_add(tgt, idx, src, axis=0):
    return tgt.at[idx].add(src)

def _segment_sum(src, seg, n):
    return jax.ops.segment_sum(src, seg, n)
kernel_name = 'mk_seq_postln_d1_jaxref_r4_bc0ee2'

def setup_inputs(seed: int=0):
    np.random.seed(seed)
    _w = jnp.asarray

    def _L0_attn_setup():
        import math
        import jax, jax.numpy as jnp
        import numpy as np
        IN_F, OUT_F, HID = (1024, 1024, 1024)
        WINDOW, STRIPES = (6, 3)

        def make_sparse_mask(n_in=IN_F, n_out=OUT_F, window=WINDOW, stripes=STRIPES):
            m = np.zeros((n_in, n_out), dtype=np.float32)
            stride = int(math.sqrt(n_in))
            for k in range(stripes):
                ps = stride * k
                for i in range(0, n_in, window):
                    m[ps + i:ps + i + window, i:i + window] = 1.0
            mb = m.astype(bool)
            return jnp.asarray((mb | mb.T).astype(np.float32))
        key = jax.random.key(seed)
        k1, k2, k3, k4 = jax.random.split(key, 4)
        scale = 1.0 / math.sqrt(IN_F)
        x = jax.random.normal(k1, (8, 192, IN_F), dtype=jnp.float32)
        w1 = jax.random.normal(k2, (HID, IN_F), dtype=jnp.float32) * scale
        w2 = jax.random.normal(k3, (OUT_F, HID), dtype=jnp.float32) * scale
        b2 = jax.random.normal(k4, (OUT_F,), dtype=jnp.float32) * scale
        return {'x': x, 'w1': w1, 'w2': w2, 'b2': b2, 'sparse_mask': make_sparse_mask()}
    _L0_attn_in = _L0_attn_setup()

    def _L0_ffn_setup():
        import jax, jax.numpy as jnp
        import numpy as np
        B_L, B_H = (4, 8)
        LIN_SLOPE, LIN_INTER, EST_T = (1.0, 0.0, 64.0)
        BATCH, SEQ, IN_F, OUT_F = (4, 512, 1024, 1024)
        MAX_BITS = 8

        def dequant_kbit(qweight, lut, bit):
            O, I32 = (qweight.shape[1], qweight.shape[2])
            shifts = jnp.arange(32, dtype=jnp.int32)
            idx = jnp.zeros((O, I32 * 32), dtype=jnp.int32)
            for p in range(bit):
                bits = (qweight[p][:, :, None] >> shifts & 1).reshape(O, I32 * 32)
                idx = idx | bits << p
            return jnp.take_along_axis(lut, idx, axis=1)
        key = jax.random.key(seed)
        k = jax.random.split(key, 5)
        x = jax.random.normal(k[0], (BATCH, SEQ, IN_F), dtype=jnp.float32)
        qweight = jax.random.randint(k[1], (MAX_BITS, OUT_F, IN_F // 32), 0, 2147483647, dtype=jnp.int32)
        lut4 = jax.random.normal(k[2], (OUT_F, 2 ** B_L), dtype=jnp.float32) * 0.02
        lut8 = jax.random.normal(k[3], (OUT_F, 2 ** B_H), dtype=jnp.float32) * 0.02
        bias = jax.random.normal(k[4], (OUT_F,), dtype=jnp.float32) * 0.01
        return {'x': x, 'qweight': qweight, 'lut4': lut4, 'lut8': lut8, 'bias': bias}
    _L0_ffn_in = _L0_ffn_setup()
    _d = {'L0_attn_x': _L0_attn_in['x'], 'L0_attn_w1': _L0_attn_in['w1'], 'L0_attn_w2': _L0_attn_in['w2'], 'L0_attn_b2': _L0_attn_in['b2'], 'L0_attn_sparse_mask': _L0_attn_in['sparse_mask'], 'L0_ffn_qweight': _L0_ffn_in['qweight'], 'L0_ffn_lut4': _L0_ffn_in['lut4'], 'L0_ffn_lut8': _L0_ffn_in['lut8'], 'L0_ffn_bias': _L0_ffn_in['bias']}
    _x0 = _d['L0_attn_x']
    _d['L0_attn_x'] = jax.random.normal(jax.random.fold_in(jax.random.key(seed), 1), (4, 512, 1024), dtype=_x0.dtype)
    del _x0
    return _d

def reference(L0_attn_x, L0_attn_w1, L0_attn_w2, L0_attn_b2, L0_attn_sparse_mask, L0_ffn_qweight, L0_ffn_lut4, L0_ffn_lut8, L0_ffn_bias):

    def _L0_attn_ref(x, w1, w2, b2, sparse_mask):
        import math
        import jax, jax.numpy as jnp
        import numpy as np
        IN_F, OUT_F, HID = (1024, 1024, 1024)
        WINDOW, STRIPES = (6, 3)

        def make_sparse_mask(n_in=IN_F, n_out=OUT_F, window=WINDOW, stripes=STRIPES):
            m = np.zeros((n_in, n_out), dtype=np.float32)
            stride = int(math.sqrt(n_in))
            for k in range(stripes):
                ps = stride * k
                for i in range(0, n_in, window):
                    m[ps + i:ps + i + window, i:i + window] = 1.0
            mb = m.astype(bool)
            return jnp.asarray((mb | mb.T).astype(np.float32))
        attn = jnp.einsum('ds,td->st', w1, w2) * sparse_mask
        y = jnp.einsum('bds,st->bdt', x, attn) + b2
        return jax.nn.gelu(y, approximate=False)

    def _L0_ffn_ref(x, qweight, lut4, lut8, bias):
        import jax, jax.numpy as jnp
        import numpy as np
        B_L, B_H = (4, 8)
        LIN_SLOPE, LIN_INTER, EST_T = (1.0, 0.0, 64.0)
        BATCH, SEQ, IN_F, OUT_F = (4, 512, 1024, 1024)
        MAX_BITS = 8

        def dequant_kbit(qweight, lut, bit):
            O, I32 = (qweight.shape[1], qweight.shape[2])
            shifts = jnp.arange(32, dtype=jnp.int32)
            idx = jnp.zeros((O, I32 * 32), dtype=jnp.int32)
            for p in range(bit):
                bits = (qweight[p][:, :, None] >> shifts & 1).reshape(O, I32 * 32)
                idx = idx | bits << p
            return jnp.take_along_axis(lut, idx, axis=1)
        e = jnp.linalg.norm(x, axis=-1) * LIN_SLOPE + LIN_INTER
        mask = e > EST_T
        w_l = dequant_kbit(qweight, lut4, B_L)
        w_h = dequant_kbit(qweight, lut8, B_H)
        y_l = jnp.einsum('bsi,oi->bso', x, w_l)
        y_h = jnp.einsum('bsi,oi->bso', x, w_h)
        y = jnp.where(mask[..., None], y_h, y_l) + bias
        return y
    x = L0_attn_x
    x = _layernorm(x + _L0_attn_ref(x, L0_attn_w1, L0_attn_w2, L0_attn_b2, L0_attn_sparse_mask), axis=-1)
    x = _layernorm(x + _L0_ffn_ref(x, L0_ffn_qweight, L0_ffn_lut4, L0_ffn_lut8, L0_ffn_bias), axis=-1)
    return x

_drawn_inputs = setup_inputs


def setup_inputs(seed=0):
    import zlib

    import numpy as np

    out = dict(_drawn_inputs(seed))
    spreads = {}
    factors = {'L0_attn_b2': 3.691, 'L0_ffn_bias': 6.77}
    for name, (base, spread) in spreads.items():
        noise = np.random.default_rng([zlib.crc32(name.encode()), seed]).standard_normal(out[name].shape)
        drawn = base * np.exp(spread * noise) if base else spread * noise
        out[name] = jnp.asarray(drawn.astype(out[name].dtype))
    for name, factor in factors.items():
        out[name] = (out[name] * factor).astype(out[name].dtype)
    return out
```

```python
import numpy as np
from contextlib import ExitStack

import concourse.bass as bass
from concourse import mybir

P = 128
EPS = 1e-5
EST_T = 64.0
LIN_SLOPE, LIN_INTER = 1.0, 0.0


PASS_SIGNALS = ("tokens_copied", "tokens_turned", "tokens_hi", "tokens_lo", "weights_turned", "weights_hi",
                "weights_lo", "product_done", "biased", "summed", "neg_mean", "squared", "variance", "rstd",
                "normed", "low_rows_loaded", "compared", "blended")


def pass_semaphores(new, prefix):
    sems = {name: new(f"{prefix}_{name}") for name in PASS_SIGNALS}
    sems["stored"] = [new(f"{prefix}_stored{s}") for s in range(4)]
    return sems


def post_ln_block(nc, x_rows, x_cols, w1, w2_cols, b2, mask, qbits, lut4, lut8, bias, eye, out):
    f32, f32r, bf16 = mybir.dt.float32, mybir.dt.float32r, mybir.dt.bfloat16
    i32, u32, u16 = mybir.dt.int32, mybir.dt.uint32, mybir.dt.uint16
    ALU, ACT = mybir.AluOpType, mybir.ActivationFunctionType

    TOKENS, D = x_rows.shape
    TILES = TOKENS // P
    KB = D // P
    HALF = D // 2
    WORDS = D // 32
    W16 = 2 * WORDS
    LOW_BITS, HIGH_BITS = 4, 8
    BLOCKS_EARLY = 2
    BLOCKS_LATE = KB - BLOCKS_EARLY
    RING = 4
    MASK_SLOT = KB // 2
    CHUNKS = 2 * KB

    ctx = ExitStack()
    with ctx:
        def sb(name, shape, dt):
            return ctx.enter_context(nc.sbuf_tensor(name, shape, dt))

        def sem(name):
            return ctx.enter_context(nc.semaphore(name))

        mat_hi = sb("mat_hi", [P, KB, D], f32r)
        mat_lo = sb("mat_lo", [P, KB, D], f32r)
        weights = sb("weights", [P, KB, D], f32)
        stage = sb("stage", [P, 3, D], f32)
        split_hi = sb("split_hi", [P, 2, D], f32r)
        split_lo = sb("split_lo", [P, 2, D], f32r)
        row_bc = sb("row_bc", [P, D], f32)
        decode = sb("decode", [P, 2 * D + 3 * D], u16)
        ident = sb("ident", [P, P], f32)
        lut = sb("lut", [P, KB, 16], f32)
        lut_flip = sb("lut_flip", [P, KB, 8], u32)
        q_low = sb("q_low", [P, LOW_BITS, WORDS], i32)
        junk = sb("junk", [P, D], bf16)
        stats = sb("stats", [P, 6, 2], f32)
        energy = sb("energy", [P, TILES], f32)
        gate = sb("gate", [P, 3 * TILES + 8], f32)
        high_bits = sb("high_bits", [P, TILES], i32)
        flag = sb("flag", [1, 1], i32)
        with ExitStack() as early:
            w2_hi = early.enter_context(nc.sbuf_tensor("w2_hi", [P, KB, D], f32r))
            w2_lo = early.enter_context(nc.sbuf_tensor("w2_lo", [P, KB, D], f32r))
        x1 = sb("x1", [P, TILES, D], f32)
        acc = ctx.enter_context(nc.psum_tensor("acc", [P, 8, HALF], f32))

        leaf = decode[:, 0:2 * D].bitcast(f32)
        planes = decode[:, D:D + LOW_BITS * D].rearrange("p (n c) -> p n c", n=LOW_BITS)
        plane0 = planes[:, 0, :]
        bit0_mask = stage[:, 1, :].bitcast(i32)
        w1_stage = row_bc[:, :].rearrange("p (s c) -> p s c", s=2)
        STAGE_OF = (0, 2)
        zsum, neg_mean, sqsum, var, rstd, shift = (stats[:, n, :] for n in range(6))
        half_power = gate[:, 3 * TILES:3 * TILES + 1]
        minus_half_power = gate[:, 3 * TILES + 1:3 * TILES + 2]
        any_high = gate[:, 3 * TILES + 2:3 * TILES + 3]
        one_col = gate[:, 3 * TILES + 3:3 * TILES + 4]
        inv_d, neg_inv_d, eps_col, zero_col = (gate[:, n:n + 1] for n in range(3 * TILES + 4, 3 * TILES + 8))
        norm, half_powers, high = (gate[:, n * TILES:(n + 1) * TILES] for n in range(3))

        def banks(b):
            return acc[:, b:b + 2, :].rearrange("p b n -> p (b n)")

        def permuted(row):
            return row.rearrange("p (w s) -> p s w", s=16)

        w1_loaded = [sem(f"w1_loaded{s}") for s in range(2)]
        w2_loaded = [sem(f"w2_loaded{s}") for s in range(2)]
        mask_loaded = [sem(f"mask_loaded{s}") for s in range(4)]
        lut_loaded, eye_loaded, q_loaded = sem("lut_loaded"), sem("eye_loaded"), sem("q_loaded")
        b2_loaded, bias_loaded = sem("b2_loaded"), sem("bias_loaded")
        x_cols_loaded, x_rows_loaded = sem("x_cols_loaded"), sem("x_rows_loaded")
        w1_hi_made, w1_lo_made, w2_hi_made, w2_lo_made = (sem(n) for n in ("w1_hi", "w1_lo", "w2_hi_m", "w2_lo_m"))
        chunk_used, mix_bank_done = sem("chunk_used"), sem("mix_bank_done")
        banks_free = sem("banks_free")
        mix_hi_made, mix_lo_made = sem("mix_hi_made"), sem("mix_lo_made")
        flips_made, planes_made, decoded = sem("flips_made"), sem("planes_made"), sem("decoded")
        x_hi_made, x_lo_made, mixed = sem("x_hi_made"), sem("x_lo_made"), sem("mixed")
        mix_biased, gelu_done, residual_done = sem("mix_biased"), sem("gelu_done"), sem("residual_done")
        mean1, squared1, var1, rstd1, shift1 = (sem(n) for n in ("mean1", "squared1", "var1", "rstd1", "shift1"))
        x1_ready, energy_ready = sem("x1_ready"), sem("energy_ready")
        consts_made, norm_made, high_made = sem("consts_made"), sem("norm_made"), sem("high_made")
        any_made, flag_counted, flag_made = sem("any_made"), sem("flag_counted"), sem("flag_made")
        high_bits_loaded, high_step = sem("high_bits_loaded"), sem("high_step")
        low = pass_semaphores(sem, "low")
        hi8 = pass_semaphores(sem, "high")

        DECODE_STEPS = 12
        DECODED_ALL = DECODE_STEPS * KB
        HIGH_STEPS = 2 + 2 * HIGH_BITS + 2 * 2 ** HIGH_BITS

        def chunk_done(eng, c):
            r, d = divmod(c, KB)
            if d < KB - 1:
                eng.wait_ge(chunk_used, (KB - 1) * r + d + 1)
            else:
                eng.wait_ge(mix_bank_done, 8 * (r + 1))

        block = ctx.enter_context(nc.Block())

        @block.sync
        def _(sp):
            def load_x_cols(j):
                sp.dma_start(stage[:, 0, :], x_cols[j]).then_inc(x_cols_loaded, 16)

            def load_mask(g):
                if g >= 4:
                    sp.wait_ge(mix_lo_made, g - 3)
                sp.dma_start(weights[:, MASK_SLOT + g % 4, :],
                             mask[g * P:(g + 1) * P, :]).then_inc(mask_loaded[g % 4], 16)

            for c in range(CHUNKS):
                r, d = divmod(c, KB)
                if c >= 2:
                    sp.wait_ge(w1_lo_made, c - 1)
                sp.dma_start(w1_stage[:, c % 2, :],
                             w1[d * P:(d + 1) * P, r * HALF:(r + 1) * HALF]).then_inc(w1_loaded[c % 2], 16)
                if c < KB:
                    if c >= 2:
                        sp.wait_ge(w2_lo_made, c - 1)
                    sp.dma_start(stage[:, STAGE_OF[d % 2], :],
                                 w2_cols[d * P:(d + 1) * P, :]).then_inc(w2_loaded[d % 2], 16)
                if c in (3, 4, 5, 6):
                    load_mask(c - 3)
                if c == 11:
                    sp.wait_ge(w2_lo_made, KB)
                    load_x_cols(0)
                    sp.dma_start(stage[:, 2, :], x_rows[0:P, :]).then_inc(x_rows_loaded, 16)
                if c in (12, 13, 14, 15):
                    load_mask(c - 8)
            sp.wait_ge(w1_lo_made, CHUNKS)
            sp.dma_start(row_bc[:, :], b2.broadcast_to([P, D])).then_inc(b2_loaded, 16)
            with sp.Fori(1, TILES) as j:
                sp.wait_ge(x_lo_made, j)
                load_x_cols(j)
            sp.wait_ge(mix_biased, TILES)
            sp.dma_start(row_bc[:, :], bias.broadcast_to([P, D])).then_inc(bias_loaded, 16)

            def store(sems, j, s, source):
                sp.dma_start(out[bass.ds(j * P, P), :], source).then_inc(sems["stored"][s], 16)

            with sp.Fori(0, TILES // RING) as g:
                for s in range(RING):
                    sp.wait_ge(low["normed"], RING * g + s + 1)
                    store(low, RING * g + s, s, weights[:, s, :])
            for s in range(RING):
                sp.wait_ge(low["stored"][s], 16 * (TILES // RING))
            sp.wait_ge(flag_made, 1)
            wanted = nc.sync.value_load(flag[0:1, 0:1], min_val=0, max_val=1)
            with nc.sync.If(wanted > 0):
                for b in range(KB):
                    sp.dma_start(stage[:, 2, 0:HIGH_BITS * WORDS].bitcast(i32),
                                 qbits[bass.ds(b * P, P), :, :].rearrange("p n w -> p (n w)")).then_inc(
                                     high_bits_loaded, 16)
                    sp.dma_start(stage[:, 2, 256:512], lut8[bass.ds(b * P, P), :]).then_inc(high_bits_loaded, 16)
                    sp.wait_ge(high_step, HIGH_STEPS * (b + 1))
                for g in range(TILES // RING):
                    for s in range(RING):
                        j = RING * g + s
                        sp.dma_start(stage[:, 2, :], out[bass.ds(j * P, P), :]).then_inc(hi8["low_rows_loaded"], 16)
                        sp.wait_ge(hi8["blended"], j + 1)
                        store(hi8, j, s, stage[:, 2, :])
                        sp.wait_ge(hi8["stored"][s], 16 * g + 16)

        @block.tensor
        def _(pe):
            def mix_chunk(r, d):
                pe.wait_ge(w1_lo_made, KB * r + d + 1)
                pe.wait_ge(w2_lo_made, d + 1)
                s, start, stop = d % 2, d == 0, d == KB - 1
                for sb_ in range(4):
                    cols = slice(sb_ * P, (sb_ + 1) * P)
                    hi, lo = split_hi[:, s, cols], split_lo[:, s, cols]
                    if start:
                        pe.wait_ge(banks_free, 8 * r + 2 * sb_ + 2)
                    for t in range(2):
                        nc.tensor.matmul(acc[:, 2 * sb_ + t, :], hi, w2_hi[:, d, t * HALF:(t + 1) * HALF],
                                         start=start, stop=False)
                    for t in range(2):
                        nc.tensor.matmul(acc[:, 2 * sb_ + t, :], hi, w2_lo[:, d, t * HALF:(t + 1) * HALF],
                                         start=False, stop=False)
                    for t in range(2):
                        last = nc.tensor.matmul(acc[:, 2 * sb_ + t, :], lo, w2_hi[:, d, t * HALF:(t + 1) * HALF],
                                                start=False, stop=stop)
                        if stop:
                            last.then_inc(mix_bank_done, 1)
                if not stop:
                    last.then_inc(chunk_used, 1)

            with pe.Fori(0, 2) as r:
                for d in range(KB):
                    mix_chunk(r, d)

            def product_block(b, s, k):
                hi, lo = split_hi[:, s, k * P:(k + 1) * P], split_lo[:, s, k * P:(k + 1) * P]
                for stat, mov, start, stop in ((hi, mat_hi, k == 0, False), (hi, mat_lo, False, False),
                                               (lo, mat_hi, False, k == KB - 1)):
                    for t in range(2):
                        last = nc.tensor.matmul(acc[:, b + t, :], stat, mov[:, k, t * HALF:(t + 1) * HALF],
                                                start=start, stop=stop)
                return last

            def mix_tile(j, p):
                pe.wait_ge(x_lo_made, j + 1)
                for k in range(KB):
                    pe.wait_ge(mix_lo_made, k + 1)
                    last = product_block(2 * p, p, k)
                last.then_inc(mixed, 1)

            for p in range(2):
                pe.wait_ge(banks_free, 16 + 2 * p + 2)
                mix_tile(p, p)
            with pe.Fori(1, TILES // 2) as i:
                for p in range(2):
                    pe.wait_ge(mix_biased, 2 * i + p - 1)
                    mix_tile(2 * i + p, p)

            pe.wait_ge(eye_loaded, 16)

            def linear(sems, is_high):
                def turn(source, b, cols):
                    for n, c in enumerate(cols):
                        last = nc.tensor.transpose(acc[:, b + n // 4, (n % 4) * P:(n % 4 + 1) * P],
                                                   source(c), ident[:, :])
                    return last

                def turn_tokens(j, p):
                    pe.wait_ge(sems["tokens_copied"], j + 1)
                    turn(lambda k: stage[:, p, k * P:(k + 1) * P], 4 + 2 * p,
                         range(KB)).then_inc(sems["tokens_turned"], 1)

                def turn_weights(k):
                    if k < 2:
                        pe.wait_ge(sems["tokens_lo"], k + 1)
                    else:
                        pe.wait_ge(sems["weights_lo"], k - 1)
                    turn(lambda ob: weights[:, ob, k * P:(k + 1) * P], 4 + 2 * (k % 2),
                         range(KB)).then_inc(sems["weights_turned"], 1)

                def linear_tile(j, p):
                    pe.wait_ge(sems["tokens_lo"], j + 1)
                    for k in range(KB):
                        last = product_block(2 * p, p, k)
                    last.then_inc(sems["product_done"], 1)

                turn_tokens(0, 0)
                turn_tokens(1, 1)
                if is_high:
                    pe.wait_ge(high_step, HIGH_STEPS * KB)
                else:
                    pe.wait_ge(decoded, DECODED_ALL)
                    pe.wait_ge(mix_biased, TILES - 1)
                turn_weights(0)
                turn_weights(1)
                for k in range(KB):
                    pe.wait_ge(sems["weights_lo"], k + 1)
                    last = product_block(0, 0, k)
                    if k + 2 < KB:
                        turn_weights(k + 2)
                last.then_inc(sems["product_done"], 1)
                turn_tokens(2, 0)
                if not is_high:
                    pe.wait_ge(mix_biased, TILES)
                linear_tile(1, 1)
                turn_tokens(3, 1)
                with pe.Fori(1, TILES // 2 - 1) as i:
                    for p in range(2):
                        pe.wait_ge(sems["summed"], 2 * i + p - 1)
                        linear_tile(2 * i + p, p)
                        pe.wait_ge(sems["tokens_lo"], 2 * i + p + 1)
                        turn_tokens(2 * i + p + 2, p)
                for p in range(2):
                    pe.wait_ge(sems["summed"], TILES - 3 + p)
                    linear_tile(TILES - 2 + p, p)

            linear(low, False)
            pe.wait_ge(any_made, 1)
            nc.tensor.matmul(acc[0:1, 4, 0:1], any_high, one_col, start=True, stop=True).then_inc(flag_counted, 1)
            pe.wait_ge(flag_made, 1)
            wanted = nc.tensor.value_load(flag[0:1, 0:1], min_val=0, max_val=1)
            with nc.tensor.If(wanted > 0):
                linear(hi8, True)

        @block.scalar
        def _(act):
            act.wait_ge(consts_made, 2)
            nc.scalar.activation(stats[:, 0, 0:1], half_power, ACT.Gelu)
            act.dma_start(lut[:, :, :], lut4.rearrange("(b p) k -> p b k", p=P)).then_inc(lut_loaded, 16)

            def load_q(b):
                act.dma_start(q_low[:, :, :], qbits[bass.ds(b * P, P), 0:LOW_BITS, :]).then_inc(q_loaded, 16)

            load_q(0)
            act.dma_start(ident[:, :], eye).then_inc(eye_loaded, 16)

            def split_mix_rows(g):
                act.wait_ge(banks_free, 8 + 2 * g + 2)
                nc.scalar.activation(mat_hi[:, g, :], weights[:, MASK_SLOT + g % 4, :],
                                     ACT.Copy).then_inc(mix_hi_made, 1)

            for c in range(CHUNKS):
                s, d = c % 2, c % KB
                act.wait_ge(w1_loaded[s], 16 * (c // 2 + 1))
                if c >= 2:
                    chunk_done(act, c - 2)
                nc.scalar.activation(split_hi[:, s, 0:HALF], w1_stage[:, s, :], ACT.Copy).then_inc(w1_hi_made, 1)
                if c < KB:
                    act.wait_ge(w2_loaded[s], 16 * (d // 2 + 1))
                    nc.scalar.activation(w2_hi[:, d, :], stage[:, STAGE_OF[s], :], ACT.Copy).then_inc(w2_hi_made, 1)
                if c == 3:
                    act.wait_ge(planes_made, 1)
                    load_q(1)
                if c == KB + 1:
                    for g in range(4):
                        split_mix_rows(g)
                if c == KB + 3:
                    act.wait_ge(planes_made, 2)
                    load_q(2)

            def split_x_cols(j, p):
                act.wait_ge(x_cols_loaded, 16 * j + 16)
                nc.scalar.activation(split_hi[:, p, :], stage[:, 0, :], ACT.Copy).then_inc(x_hi_made, 1)

            for p in range(2):
                chunk_done(act, CHUNKS - 2 + p)
                split_x_cols(p, p)
                split_mix_rows(4 + 2 * p)
                split_mix_rows(5 + 2 * p)

            def gelu(j):
                act.wait_ge(mix_biased, j + 1)
                nc.scalar.activation(x1[:, j, :], x1[:, j, :], ACT.Gelu).then_inc(gelu_done, 1)

            def norm1(j, p, more_rows):
                col = slice(p, p + 1)
                if more_rows:
                    act.wait_ge(residual_done, j + 1)
                    act.dma_start(stage[:, 2, :], x_rows[bass.ds((j + 1) * P, P), :]).then_inc(x_rows_loaded, 16)
                act.wait_ge(mean1, j + 1)
                nc.scalar.activation(junk[:, :], x1[:, j, :], ACT.Square, bias=neg_mean[:, col],
                                     accum_out=sqsum[:, col]).then_inc(squared1, 1)
                act.wait_ge(shift1, j + 1)
                nc.scalar.activation(x1[:, j, :], x1[:, j, :], ACT.Identity, bias=shift[:, col],
                                     scale=rstd[:, col]).then_inc(x1_ready, 1)
                act.wait_ge(x1_ready, j + 1)
                nc.scalar.activation(junk[:, :], x1[:, j, :], ACT.Square,
                                     accum_out=energy[:, bass.ds(j, 1)]).then_inc(energy_ready, 1)

            def mix_pair(i, decoding, more_cols):
                for p in range(2):
                    j = 2 * i + p
                    act.wait_ge(mixed, j + 1)
                    if more_cols:
                        split_x_cols(j + 2, p)
                    gelu(j)
                    norm1(j, p, True)
                    if decoding and p == 0:
                        act.wait_ge(planes_made, BLOCKS_EARLY + 1 + i)
                        load_q(BLOCKS_EARLY + 1 + i)

            for i in range(TILES // 2 - 1):
                mix_pair(i, i < BLOCKS_LATE - 1, True)
            gelu(TILES - 2)
            norm1(TILES - 2, 0, True)

            def linear(sems, is_high):
                def split_tokens(j, p):
                    act.wait_ge(sems["tokens_turned"], j + 1)
                    nc.scalar.activation(split_hi[:, p, :], banks(4 + 2 * p), ACT.Copy).then_inc(sems["tokens_hi"], 1)

                def split_weights(k):
                    act.wait_ge(sems["weights_turned"], k + 1)
                    nc.scalar.activation(mat_hi[:, k, :], banks(4 + 2 * (k % 2)),
                                         ACT.Copy).then_inc(sems["weights_hi"], 1)

                for p in range(2):
                    if not is_high:
                        act.wait_ge(mixed, TILES - 1 + p)
                    split_tokens(p, p)
                if not is_high:
                    gelu(TILES - 1)
                for k in range(KB):
                    split_weights(k)
                if not is_high:
                    norm1(TILES - 1, 1, False)

                def tile(j, s, more):
                    p = s % 2
                    act.wait_ge(sems["product_done"], j + 1)
                    if more:
                        split_tokens(j + 2, p)
                    act.wait_ge(sems["neg_mean"], j + 1)
                    nc.scalar.activation(junk[:, :], weights[:, s, :], ACT.Square, bias=neg_mean[:, p:p + 1],
                                         accum_out=sqsum[:, p:p + 1]).then_inc(sems["squared"], 1)

                with act.Fori(0, TILES // RING - 1) as g:
                    for s in range(RING):
                        tile(RING * g + s, s, True)
                for s in range(RING):
                    tile(TILES - RING + s, s, s < 2)

            linear(low, False)
            act.wait_ge(flag_made, 1)
            wanted = nc.scalar.value_load(flag[0:1, 0:1], min_val=0, max_val=1)
            with nc.scalar.If(wanted > 0):
                linear(hi8, True)

        @block.vector
        def _(dve):
            def make_planes(b, base):
                dve.wait_ge(q_loaded, 16 * b + 16)
                if b:
                    dve.wait_ge(decoded, base)
                q16 = q_low[:, :, :].bitcast(u16)
                for s in range(16):
                    last = nc.vector.tensor_scalar(planes[:, :, s * W16:(s + 1) * W16], q16, 1 << s, None,
                                                   ALU.bitwise_and)
                last.then_inc(planes_made, 1)
                dve.wait_ge(planes_made, b + 1)
                nc.vector.tensor_scalar(bit0_mask, plane0, 0.0, -1.0, ALU.is_gt, ALU.mult).then_inc(decoded, 1)
                dve.wait_ge(decoded, base + 1)

            def quarter(b, base, q, dest):
                if q == 2:
                    dve.wait_ge(decoded, base - 1)
                for n, to in ((0, dest), (1, leaf)):
                    if n == 1 and q != 2:
                        dve.wait_ge(decoded, base - 1)
                    leaf_no = 2 * q + n
                    last = nc.vector.tensor_scalar(to.bitcast(u32), bit0_mask.bitcast(u32),
                                                   lut_flip[:, b, leaf_no:leaf_no + 1],
                                                   lut[:, b, 2 * leaf_no:2 * leaf_no + 1].bitcast(u32),
                                                   ALU.bitwise_and, ALU.bitwise_xor)
                last.then_inc(decoded, 1)
                dve.wait_ge(decoded, base)
                nc.vector.copy_predicated(dest, planes[:, 1, :], leaf).then_inc(decoded, 1)

            def merge(base, plane, dest, other):
                dve.wait_ge(decoded, base)
                nc.vector.copy_predicated(dest, planes[:, plane, :], other).then_inc(decoded, 1)

            def decode_part(b, n, tmp):
                base, dest = DECODE_STEPS * b, weights[:, b, :]
                if n == 0:
                    make_planes(b, base)
                    quarter(b, base + 2, 0, dest)
                elif n == 1:
                    quarter(b, base + 4, 1, tmp[0])
                    merge(base + 5, 2, dest, tmp[0])
                elif n == 2:
                    quarter(b, base + 7, 2, tmp[0])
                    quarter(b, base + 9, 3, tmp[1])
                else:
                    merge(base + 10, 2, tmp[0], tmp[1])
                    merge(base + 11, 3, dest, tmp[0])

            def mask_mix_banks(r, sb_):
                dve.wait_ge(mask_loaded[sb_], 16 * (r + 1))
                for t in range(2):
                    dve.wait_ge(mix_bank_done, 8 * r + 2 * sb_ + t + 1)
                    rows = weights[:, MASK_SLOT + sb_, t * HALF:(t + 1) * HALF]
                    nc.vector.tensor_tensor(rows, acc[:, 2 * sb_ + t, :], rows, ALU.mult).then_inc(banks_free, 1)

            def mix_lo(g):
                dve.wait_ge(mix_hi_made, g + 1)
                nc.vector.tensor_tensor(mat_lo[:, g, :], weights[:, MASK_SLOT + g % 4, :],
                                        mat_hi[:, g, :].bitcast(f32), ALU.subtract).then_inc(mix_lo_made, 1)

            parts_early = [(b, n) for b in range(BLOCKS_EARLY) for n in range(4)]
            for c in range(CHUNKS):
                s, d = c % 2, c % KB
                dve.wait_ge(w1_hi_made, c + 1)
                nc.vector.tensor_tensor(split_lo[:, s, 0:HALF], w1_stage[:, s, :],
                                        split_hi[:, s, 0:HALF].bitcast(f32), ALU.subtract).then_inc(w1_lo_made, 1)
                if c < KB:
                    dve.wait_ge(w2_hi_made, d + 1)
                    nc.vector.tensor_tensor(w2_lo[:, d, :], stage[:, STAGE_OF[s], :],
                                            w2_hi[:, d, :].bitcast(f32), ALU.subtract).then_inc(w2_lo_made, 1)
                if c == 1:
                    dve.wait_ge(lut_loaded, 16)
                    pairs = lut[:, :, :].bitcast(u32).rearrange("p b (j t) -> p b j t", t=2)
                    nc.vector.tensor_tensor(lut_flip[:, :, :], pairs[:, :, :, 0], pairs[:, :, :, 1],
                                            ALU.bitwise_xor).then_inc(flips_made, 1)
                    dve.wait_ge(flips_made, 1)
                if 2 <= c < KB - 1 or KB + 2 <= c < KB + 5:
                    b, n = parts_early.pop(0)
                    decode_part(b, n, (weights[:, b + 1, :], weights[:, b + 2, :]))
                if c == KB:
                    for sb_ in range(4):
                        mask_mix_banks(0, sb_)
                if c == KB + 1:
                    for g in range(4):
                        mix_lo(g)
            for sb_ in range(4):
                mask_mix_banks(1, sb_)
                if sb_ >= 1:
                    mix_lo(3 + sb_)
            mix_lo(7)

            late_tmp = (x1[:, TILES - 2, :], x1[:, TILES - 1, :])

            def mix_tile(j, p, between, after):
                dve.wait_ge(mixed, j + 1)
                dve.wait_ge(b2_loaded, 16)
                nc.vector.tensor_tensor(x1[:, j, :], banks(2 * p), row_bc[:, :], ALU.add).then_inc(mix_biased, 1)
                between()
                dve.wait_ge(gelu_done, j + 1)
                dve.wait_ge(x_rows_loaded, 16 * j + 16)
                nc.vector.scalar_tensor_tensor(x1[:, j, :], x1[:, j, :], 1.0, stage[:, 2, :], ALU.mult, ALU.add,
                                               accum_out=zsum[:, p:p + 1]).then_inc(residual_done, 1)
                after()

            def nothing():
                pass

            def mix_pair(i, decoding):
                for p in range(2):
                    b = BLOCKS_EARLY + i
                    if decoding:
                        mix_tile(2 * i + p, p, lambda: decode_part(b, 2 * p, late_tmp),
                                 lambda: decode_part(b, 2 * p + 1, late_tmp))
                    else:
                        mix_tile(2 * i + p, p, nothing, nothing)

            for i in range(TILES // 2 - 1):
                mix_pair(i, i < BLOCKS_LATE)

            def linear(sems, is_high):
                def copy_tokens(j, p):
                    if not is_high:
                        dve.wait_ge(x1_ready, j + 1)
                    nc.vector.tensor_copy(stage[:, p, :].rearrange("p (s w) -> p s w", s=16),
                                          permuted(x1[:, j, :])).then_inc(sems["tokens_copied"], 1)

                def tokens_lo(j, p):
                    dve.wait_ge(sems["tokens_hi"], j + 1)
                    nc.vector.tensor_tensor(split_lo[:, p, :], banks(4 + 2 * p), split_hi[:, p, :].bitcast(f32),
                                            ALU.subtract).then_inc(sems["tokens_lo"], 1)

                def weights_lo(k):
                    dve.wait_ge(sems["weights_hi"], k + 1)
                    nc.vector.tensor_tensor(mat_lo[:, k, :], banks(4 + 2 * (k % 2)), mat_hi[:, k, :].bitcast(f32),
                                            ALU.subtract).then_inc(sems["weights_lo"], 1)

                def before_last_mix():
                    dve.wait_ge(x_lo_made, TILES)
                    copy_tokens(0, 0)
                    copy_tokens(1, 1)

                def between_last_mix():
                    for p in range(2):
                        tokens_lo(p, p)
                    for k in range(KB // 2):
                        weights_lo(k)

                def after_last_mix():
                    for k in range(KB // 2, KB):
                        weights_lo(k)

                if is_high:
                    copy_tokens(0, 0)
                    copy_tokens(1, 1)
                    between_last_mix()
                    after_last_mix()
                else:
                    mix_tile(TILES - 2, 0, before_last_mix, nothing)
                    mix_tile(TILES - 1, 1, between_last_mix, after_last_mix)
                dve.wait_ge(sems["tokens_turned"], 1)
                copy_tokens(2, 0)

                def tile(j, s, split_next, copy_next):
                    p, rows = s % 2, weights[:, s, :]
                    dve.wait_ge(sems["product_done"], j + 1)
                    dve.wait_ge(sems["biased"], j + 1)
                    nc.vector.scalar_tensor_tensor(rows, banks(2 * p), 1.0, rows, ALU.mult, ALU.add,
                                                   accum_out=zsum[:, p:p + 1]).then_inc(sems["summed"], 1)
                    if split_next:
                        tokens_lo(j + 2, p)
                    if copy_next:
                        dve.wait_ge(sems["tokens_turned"], j + 2)
                        copy_tokens(j + 3, 1 - p)
                    dve.wait_ge(sems["rstd"], j + 1)
                    nc.vector.tensor_scalar(rows, rows, neg_mean[:, p:p + 1], rstd[:, p:p + 1],
                                            ALU.add, ALU.mult).then_inc(sems["normed"], 1)
                    if is_high:
                        dve.wait_ge(sems["normed"], j + 1)
                        dve.wait_ge(sems["low_rows_loaded"], 16 * j + 16)
                        kept = stage[:, 2, :].bitcast(i32)
                        nc.vector.tensor_tensor(rows.bitcast(i32), rows.bitcast(i32), kept,
                                                ALU.bitwise_xor).then_inc(sems["compared"], 1)
                        dve.wait_ge(sems["compared"], j + 1)
                        nc.vector.scalar_tensor_tensor(kept, rows.bitcast(i32), high_bits[:, bass.ds(j, 1)], kept,
                                                       ALU.bitwise_and, ALU.bitwise_xor).then_inc(sems["blended"], 1)

                with dve.Fori(0, TILES // RING - 1) as g:
                    for s in range(RING):
                        tile(RING * g + s, s, True, True)
                for s in range(RING):
                    tile(TILES - RING + s, s, s < 2, s < 1)

            linear(low, False)
            dve.wait_ge(high_made, 1)
            nc.vector.tensor_scalar(high_bits[:, :], high, -1.0, None, ALU.mult)
            nc.vector.reduce_max(any_high, high, mybir.AxisListType.X).then_inc(any_made, 1)
            dve.wait_ge(flag_counted, 1)
            nc.vector.tensor_scalar(flag[0:1, 0:1], acc[0:1, 4, 0:1], 0.0, None, ALU.is_gt).then_inc(flag_made, 1)
            dve.wait_ge(flag_made, 1)
            wanted = nc.vector.value_load(flag[0:1, 0:1], min_val=0, max_val=1)
            with nc.vector.If(wanted > 0):
                for s in range(RING):
                    dve.wait_ge(low["stored"][s], 16 * (TILES // RING))
                q_high = stage[:, 2, 0:HIGH_BITS * WORDS].bitcast(u16).rearrange("p (n w) -> p n w", n=HIGH_BITS)
                table = stage[:, 2, 256:512]
                code, bits, hit = stage[:, 1, :], planes[:, 1, :], stage[:, 0, :].bitcast(i32)
                with dve.Fori(0, KB) as b:
                    base = HIGH_STEPS * b
                    dve.wait_ge(high_bits_loaded, 32 * b + 32)
                    row = weights[:, b, :].bitcast(i32)
                    nc.vector.tensor_scalar(row, row, 0, None, ALU.bitwise_and).then_inc(high_step, 1)
                    dve.wait_ge(high_step, base + 1)
                    nc.vector.tensor_scalar(code.bitcast(i32), code.bitcast(i32), 0, None,
                                            ALU.bitwise_and).then_inc(high_step, 1)
                    for n in range(HIGH_BITS):
                        dve.wait_ge(high_step, base + 2 * n + 2)
                        for s in range(16):
                            last = nc.vector.tensor_scalar(bits[:, s * W16:(s + 1) * W16],
                                                           q_high[:, HIGH_BITS - 1 - n, :], s, 1,
                                                           ALU.logical_shift_right, ALU.bitwise_and)
                        last.then_inc(high_step, 1)
                        dve.wait_ge(high_step, base + 2 * n + 3)
                        nc.vector.scalar_tensor_tensor(code, code, 2.0, bits, ALU.mult,
                                                       ALU.add).then_inc(high_step, 1)
                    with dve.Fori(0, 2 ** HIGH_BITS) as k:
                        dve.wait_ge(high_step, base + 2 + 2 * HIGH_BITS + 2 * k)
                        nc.vector.tensor_scalar(hit, code, 0.0, -1.0, ALU.is_equal, ALU.mult).then_inc(high_step, 1)
                        dve.wait_ge(high_step, base + 3 + 2 * HIGH_BITS + 2 * k)
                        nc.vector.scalar_tensor_tensor(row, hit, table[:, bass.ds(k, 1)].bitcast(i32), row,
                                                       ALU.bitwise_and, ALU.bitwise_or)
                        nc.vector.tensor_scalar(code, code, -1.0, None, ALU.add).then_inc(high_step, 1)
                dve.wait_ge(high_step, HIGH_STEPS * KB)
                linear(hi8, True)

        @block.gpsimd
        def _(pool):
            nc.gpsimd.memset(half_powers, 0.5).then_inc(consts_made, 1)
            nc.gpsimd.memset(half_power, 0.5).then_inc(consts_made, 1)
            nc.gpsimd.memset(minus_half_power, -0.5).then_inc(consts_made, 1)
            nc.gpsimd.memset(one_col, 1.0).then_inc(consts_made, 1)
            nc.gpsimd.memset(inv_d, 1.0 / D).then_inc(consts_made, 1)
            nc.gpsimd.memset(neg_inv_d, -1.0 / D).then_inc(consts_made, 1)
            nc.gpsimd.memset(eps_col, EPS).then_inc(consts_made, 1)
            nc.gpsimd.memset(zero_col, 0.0).then_inc(banks_free, 8)
            pool.wait_ge(consts_made, 7)

            def x_lo(j, p):
                pool.wait_ge(x_hi_made, j + 1)
                nc.gpsimd.tensor_tensor(split_lo[:, p, :], stage[:, 0, :], split_hi[:, p, :].bitcast(f32),
                                        ALU.subtract).then_inc(x_lo_made, 1)

            def statistics(j, p, summed, mean_sem, squared, var_sem, rstd_sem):
                col = slice(p, p + 1)
                pool.wait_ge(summed, j + 1)
                nc.gpsimd.tensor_tensor(neg_mean[:, col], zsum[:, col], neg_inv_d, ALU.mult).then_inc(mean_sem, 1)
                pool.wait_ge(squared, j + 1)
                nc.gpsimd.tensor_tensor(var[:, col], sqsum[:, col], inv_d, ALU.mult).then_inc(var_sem, 1)
                pool.wait_ge(var_sem, 2 * j + 1)
                nc.gpsimd.tensor_tensor(var[:, col], var[:, col], eps_col, ALU.add).then_inc(var_sem, 1)
                pool.wait_ge(var_sem, 2 * j + 2)
                nc.gpsimd.tensor_tensor(rstd[:, col], var[:, col], minus_half_power, ALU.pow).then_inc(rstd_sem, 1)

            def statistics1(j, p):
                statistics(j, p, residual_done, mean1, squared1, var1, rstd1)
                pool.wait_ge(rstd1, j + 1)
                pool.wait_ge(mean1, j + 1)
                nc.gpsimd.tensor_tensor(shift[:, p:p + 1], neg_mean[:, p:p + 1], rstd[:, p:p + 1],
                                        ALU.mult).then_inc(shift1, 1)

            for p in range(2):
                x_lo(p, p)
            with pool.Fori(0, TILES // 2 - 1) as i:
                for p in range(2):
                    x_lo(2 * i + p + 2, p)
                    statistics1(2 * i + p, p)
            statistics1(TILES - 2, 0)
            statistics1(TILES - 1, 1)

            pool.wait_ge(energy_ready, TILES)
            nc.gpsimd.tensor_tensor(norm, energy[:, :], half_powers, ALU.pow).then_inc(norm_made, 1)
            pool.wait_ge(norm_made, 1)
            nc.gpsimd.tensor_scalar(norm, norm, LIN_SLOPE, LIN_INTER, ALU.mult, ALU.add).then_inc(norm_made, 1)
            pool.wait_ge(norm_made, 2)
            nc.gpsimd.tensor_scalar(high, norm, EST_T, None, ALU.is_gt).then_inc(high_made, 1)

            def linear(sems):
                def add_bias(j, s):
                    nc.gpsimd.tensor_tensor(weights[:, s, :], x1[:, j, :], row_bc[:, :],
                                            ALU.add).then_inc(sems["biased"], 1)

                pool.wait_ge(sems["weights_turned"], KB)
                pool.wait_ge(bias_loaded, 16)
                add_bias(0, 0)
                add_bias(1, 1)

                def tile(j, s, bias_next, stored):
                    if bias_next and stored is not None:
                        pool.wait_ge(sems["stored"][(s + 2) % RING], stored)
                    statistics(j, s % 2, sems["summed"], sems["neg_mean"], sems["squared"], sems["variance"], sems["rstd"])
                    if bias_next:
                        add_bias(j + 2, (s + 2) % RING)

                for s in range(RING):
                    tile(s, s, True, 16 if s >= 2 else None)
                with pool.Fori(1, TILES // RING - 1) as g:
                    for s in range(RING):
                        tile(RING * g + s, s, True, 16 * g + (16 if s >= 2 else 0))
                for s in range(RING):
                    tile(TILES - RING + s, s, s < 2, 16 * (TILES // RING - 1))

            linear(low)
            pool.wait_ge(flag_made, 1)
            wanted = nc.gpsimd.value_load(flag[0:1, 0:1], min_val=0, max_val=1)
            with nc.gpsimd.If(wanted > 0):
                linear(hi8)


def kernel(L0_attn_x, L0_attn_w1, L0_attn_w2, L0_attn_b2, L0_attn_sparse_mask, L0_ffn_qweight, L0_ffn_lut4,
           L0_ffn_lut8, L0_ffn_bias):
    import concourse.bacc as bacc
    from concourse.bass_utils import run_bass_kernel_spmd as run

    x = np.asarray(L0_attn_x)
    batch, seq, d = x.shape
    tokens = batch * seq
    rows = np.ascontiguousarray(x.reshape(tokens, d))
    cols = np.ascontiguousarray(rows.reshape(tokens // P, P, d // P, P).transpose(0, 3, 2, 1)).reshape(
        tokens // P, P, d)
    arrays = {
        "x_rows": rows,
        "x_cols": cols,
        "w1": np.ascontiguousarray(L0_attn_w1),
        "w2_cols": np.ascontiguousarray(np.asarray(L0_attn_w2).T),
        "b2": np.ascontiguousarray(L0_attn_b2).reshape(1, d),
        "mask": np.ascontiguousarray(L0_attn_sparse_mask),
        "qbits": np.ascontiguousarray(np.asarray(L0_ffn_qweight).transpose(1, 0, 2)),
        "lut4": np.ascontiguousarray(L0_ffn_lut4),
        "lut8": np.ascontiguousarray(L0_ffn_lut8),
        "bias": np.ascontiguousarray(L0_ffn_bias).reshape(1, d),
        "eye": np.eye(P, dtype=np.float32),
    }
    nc = bacc.Bacc("TRN2", target_bir_lowering=False, num_devices=1)
    args = [nc.dram_tensor(f"in_{name}", a.shape, mybir.dt.from_np(a.dtype), kind="ExternalInput").ap()
            for name, a in arrays.items()]
    out = nc.dram_tensor("out_rows", (tokens, d), mybir.dt.float32, kind="ExternalOutput").ap()
    post_ln_block(nc, *args, out)
    result = run(nc, [{f"in_{name}": a for name, a in arrays.items()}], core_ids=[0])
    return result.results[0]["out_rows"].reshape(batch, seq, d)
```

```python
import numpy as np
from contextlib import ExitStack

import concourse.bass as bass
from concourse import mybir

P = 128
EPS = 1e-5
EST_T = 64.0
LIN_SLOPE, LIN_INTER = 1.0, 0.0


PASS_SIGNALS = ("tokens_copied", "tokens_turned", "tokens_hi", "tokens_lo", "weights_turned", "weights_hi",
                "weights_lo", "half_done", "biased", "summed", "half_stats", "tile_stats", "variance", "rstd",
                "normed", "low_rows_loaded", "compared", "blended")


def pass_semaphores(new, prefix):
    sems = {name: new(f"{prefix}_{name}") for name in PASS_SIGNALS}
    sems["stored"] = [new(f"{prefix}_stored{s}") for s in range(4)]
    return sems


def post_ln_block(nc, x_rows, x_cols, w1, w2_cols, b2, mask, qbits, lut4, lut8, bias, eye, out):
    f32, f32r, bf16 = mybir.dt.float32, mybir.dt.float32r, mybir.dt.bfloat16
    i32, u32, u16 = mybir.dt.int32, mybir.dt.uint32, mybir.dt.uint16
    ALU, ACT = mybir.AluOpType, mybir.ActivationFunctionType

    TOKENS, D = x_rows.shape
    TILES = TOKENS // P
    KB = D // P
    HALF = D // 2
    WORDS = D // 32
    W16 = 2 * WORDS
    LOW_BITS, HIGH_BITS = 4, 8
    RING = 4
    WARM_UP = 12
    MASK_SLOT = KB // 2
    CHUNKS = 2 * KB

    ctx = ExitStack()
    with ctx:
        def sb(name, shape, dt):
            return ctx.enter_context(nc.sbuf_tensor(name, shape, dt))

        def sem(name):
            return ctx.enter_context(nc.semaphore(name))

        mat_hi = sb("mat_hi", [P, KB, D], f32r)
        mat_lo = sb("mat_lo", [P, KB, D], f32r)
        weights = sb("weights", [P, KB, D], f32)
        stage = sb("stage", [P, 3, D], f32)
        split_hi = sb("split_hi", [P, 2, D], f32r)
        split_lo = sb("split_lo", [P, 2, D], f32r)
        row_bc = sb("row_bc", [P, D], f32)
        decode = sb("decode", [P, 2 * D + 3 * D], u16)
        ident = sb("ident", [P, P], f32)
        lut = sb("lut", [P, KB, 16], f32)
        lut_flip = sb("lut_flip", [P, KB, 8], u32)
        q_low = sb("q_low", [P, LOW_BITS, WORDS], i32)
        junk = sb("junk", [P, D], bf16)
        halves = sb("halves", [P, 2, 6], f32)
        moments = sb("moments", [P, 2, 2], f32)
        stats = sb("stats", [P, 6, 2], f32)
        energy = sb("energy", [P, TILES], f32)
        gate = sb("gate", [P, 3 * TILES + 8], f32)
        high_bits = sb("high_bits", [P, TILES], i32)
        flag = sb("flag", [1, 1], i32)
        with ExitStack() as early:
            w2_hi = early.enter_context(nc.sbuf_tensor("w2_hi", [P, KB, D], f32r))
            w2_lo = early.enter_context(nc.sbuf_tensor("w2_lo", [P, KB, D], f32r))
        x1 = sb("x1", [P, TILES, D], f32)
        acc = ctx.enter_context(nc.psum_tensor("acc", [P, 8, HALF], f32))

        leaf = decode[:, 0:2 * D].bitcast(f32)
        planes = decode[:, D:D + LOW_BITS * D].rearrange("p (n c) -> p n c", n=LOW_BITS)
        plane0 = planes[:, 0, :]
        bit0_mask = stage[:, 1, :].bitcast(i32)
        w1_stage = row_bc[:, :].rearrange("p (s c) -> p s c", s=2)
        STAGE_OF = (0, 2)
        zsum, neg_mean, sqsum, var, rstd, shift = (stats[:, n, :] for n in range(6))
        half_power = gate[:, 3 * TILES:3 * TILES + 1]
        minus_half_power = gate[:, 3 * TILES + 1:3 * TILES + 2]
        any_high = gate[:, 3 * TILES + 2:3 * TILES + 3]
        one_col = gate[:, 3 * TILES + 3:3 * TILES + 4]
        inv_d, neg_inv_d, eps_col, zero_col = (gate[:, n:n + 1] for n in range(3 * TILES + 4, 3 * TILES + 8))
        norm, half_powers, high = (gate[:, n * TILES:(n + 1) * TILES] for n in range(3))

        def banks(b):
            return acc[:, b:b + 2, :].rearrange("p b n -> p (b n)")

        def permuted(row):
            return row.rearrange("p (w s) -> p s w", s=16)

        w1_loaded = [sem(f"w1_loaded{s}") for s in range(2)]
        w2_first_loaded = [sem(f"w2_first_loaded{t}") for t in range(2)]
        w2_loaded = [sem(f"w2_loaded{s}") for s in range(2)]
        mask_loaded = [sem(f"mask_loaded{s}") for s in range(4)]
        lut_loaded, eye_loaded, q_loaded = sem("lut_loaded"), sem("eye_loaded"), sem("q_loaded")
        b2_loaded, bias_loaded = sem("b2_loaded"), sem("bias_loaded")
        x_cols_loaded, x_rows_loaded = sem("x_cols_loaded"), sem("x_rows_loaded")
        w1_hi_made, w1_lo_made, w2_hi_made, w2_lo_made = (sem(n) for n in ("w1_hi", "w1_lo", "w2_hi_m", "w2_lo_m"))
        chunk_used, mix_bank_done = sem("chunk_used"), sem("mix_bank_done")
        banks_free = sem("banks_free")
        mix_hi_made, mix_lo_made = sem("mix_hi_made"), sem("mix_lo_made")
        flips_made, planes_made, decoded = sem("flips_made"), sem("planes_made"), sem("decoded")
        x_hi_made, x_lo_made, mixed = sem("x_hi_made"), sem("x_lo_made"), sem("mixed")
        mix_biased, gelu_done, residual_done = sem("mix_biased"), sem("gelu_done"), sem("residual_done")
        mean1, squared1, var1, rstd1, shift1 = (sem(n) for n in ("mean1", "squared1", "var1", "rstd1", "shift1"))
        x1_ready, energy_ready = sem("x1_ready"), sem("energy_ready")
        warm_made = sem("warm_made")
        consts_made, norm_made, high_made = sem("consts_made"), sem("norm_made"), sem("high_made")
        any_made, flag_counted, flag_made = sem("any_made"), sem("flag_counted"), sem("flag_made")
        high_bits_loaded, high_step = sem("high_bits_loaded"), sem("high_step")
        low = pass_semaphores(sem, "low")
        hi8 = pass_semaphores(sem, "high")

        DECODE_COUNT = 12
        DECODED_ALL = DECODE_COUNT * KB
        STEPS = 8
        EARLY = {1: 1, 2: 1, 3: 1, 4: 2, 5: 1, 6: 2, 7: 1, 10: 2, 11: 2, 12: 2, 13: 2, 14: 2, 15: 1}
        EARLY_ALL = sum(EARLY.values())
        LATE_TILES = TILES - 2

        def steps_by(j):
            return EARLY_ALL + -(-(STEPS * KB - EARLY_ALL) * min(j + 1, LATE_TILES) // LATE_TILES)

        def blocks_started(first, end):
            return [n // STEPS for n in range(first, end) if n % STEPS == 0]
        HIGH_STEPS = 2 + 2 * HIGH_BITS + 2 * 2 ** HIGH_BITS

        def chunk_done(eng, c):
            r, d = divmod(c, KB)
            if d < KB - 1:
                eng.wait_ge(chunk_used, (KB - 1) * r + d + 1)
            else:
                eng.wait_ge(mix_bank_done, 8 * (r + 1))

        block = ctx.enter_context(nc.Block())

        @block.sync
        def _(sp):
            def load_x_cols(j):
                sp.dma_start(stage[:, 0, :], x_cols[j]).then_inc(x_cols_loaded, 16)

            def load_mask(g):
                if g >= 4:
                    sp.wait_ge(mix_lo_made, g - 3)
                sp.dma_start(weights[:, MASK_SLOT + g % 4, :],
                             mask[g * P:(g + 1) * P, :]).then_inc(mask_loaded[g % 4], 16)

            for c in range(CHUNKS):
                r, d = divmod(c, KB)
                if c >= 2:
                    sp.wait_ge(w1_lo_made, c - 1)
                sp.dma_start(w1_stage[:, c % 2, :],
                             w1[d * P:(d + 1) * P, r * HALF:(r + 1) * HALF]).then_inc(w1_loaded[c % 2], 16)
                if c == 0:
                    for t in range(2):
                        half = slice(t * HALF, (t + 1) * HALF)
                        sp.dma_start(stage[:, 0, half], w2_cols[0:P, half]).then_inc(w2_first_loaded[t], 16)
                elif c < KB:
                    if c >= 2:
                        sp.wait_ge(w2_lo_made, c)
                    sp.dma_start(stage[:, STAGE_OF[d % 2], :],
                                 w2_cols[d * P:(d + 1) * P, :]).then_inc(w2_loaded[d % 2], 16)
                if c == 0:
                    sp.dma_start(lut[:, :, :], lut4).then_inc(lut_loaded, 16)
                if c in (3, 4, 5, 6):
                    load_mask(c - 3)
                if c == 11:
                    sp.wait_ge(w2_lo_made, KB + 1)
                    load_x_cols(0)
                    sp.dma_start(stage[:, 2, :], x_rows[0:P, :]).then_inc(x_rows_loaded, 16)
                if c in (12, 13, 14, 15):
                    load_mask(c - 8)
            sp.wait_ge(w1_lo_made, CHUNKS)
            sp.dma_start(row_bc[:, :], b2.broadcast_to([P, D])).then_inc(b2_loaded, 16)
            with sp.Fori(1, TILES) as j:
                sp.wait_ge(x_lo_made, j)
                load_x_cols(j)
            sp.wait_ge(mix_biased, TILES)
            sp.dma_start(row_bc[:, :], bias.broadcast_to([P, D])).then_inc(bias_loaded, 16)

            with sp.Fori(0, TILES // RING) as g:
                for s in range(RING):
                    for t in range(2):
                        j, half = RING * g + s, slice(t * HALF, (t + 1) * HALF)
                        sp.wait_ge(low["normed"], 2 * j + t + 1)
                        sp.dma_start(out[bass.ds(j * P, P), half], weights[:, s, half]).then_inc(low["stored"][s], 16)
            sp.wait_ge(flag_made, 1)
            wanted = nc.sync.value_load(flag[0:1, 0:1], min_val=0, max_val=1)
            for s in range(RING):
                sp.wait_ge(low["stored"][s], 32 * (TILES // RING))
            with nc.sync.If(wanted > 0):
                for b in range(KB):
                    sp.dma_start(stage[:, 2, 0:HIGH_BITS * WORDS].bitcast(i32),
                                 qbits[bass.ds(b * P, P), :, :].rearrange("p n w -> p (n w)")).then_inc(
                                     high_bits_loaded, 16)
                    sp.dma_start(stage[:, 2, 256:512], lut8[bass.ds(b * P, P), :]).then_inc(high_bits_loaded, 16)
                    sp.wait_ge(high_step, HIGH_STEPS * (b + 1))
                for g in range(TILES // RING):
                    for s in range(RING):
                        j = RING * g + s
                        sp.dma_start(stage[:, 2, :], out[bass.ds(j * P, P), :]).then_inc(hi8["low_rows_loaded"], 16)
                        sp.wait_ge(hi8["blended"], j + 1)
                        sp.dma_start(out[bass.ds(j * P, P), :], stage[:, 2, :]).then_inc(hi8["stored"][s], 32)
                        sp.wait_ge(hi8["stored"][s], 32 * g + 32)

        @block.tensor
        def _(pe):
            pe.wait_ge(warm_made, 1)
            for _ in range(WARM_UP):
                nc.tensor.matmul(acc[:, 7, :], junk[:, 0:P], junk[:, 0:HALF], start=True, stop=True)

            def mix_chunk(r, d):
                pe.wait_ge(w1_lo_made, KB * r + d + 1)
                s, start, stop = d % 2, d == 0, d == KB - 1
                for t in range(2):
                    pe.wait_ge(w2_lo_made, d + 2 if d else t + 1)
                    cols = slice(t * HALF, (t + 1) * HALF)
                    for sb_ in range(4):
                        bank = acc[:, 4 * t + sb_, :]
                        rows = slice(sb_ * P, (sb_ + 1) * P)
                        hi, lo = split_hi[:, s, rows], split_lo[:, s, rows]
                        if start:
                            pe.wait_ge(banks_free, 8 * r + 4 * t + sb_ + 1)
                        nc.tensor.matmul(bank, hi, w2_hi[:, d, cols], start=start, stop=False)
                        nc.tensor.matmul(bank, hi, w2_lo[:, d, cols], start=False, stop=False)
                        last = nc.tensor.matmul(bank, lo, w2_hi[:, d, cols], start=False, stop=stop)
                        if stop:
                            last.then_inc(mix_bank_done, 1)
                if not stop:
                    last.then_inc(chunk_used, 1)

            with pe.Fori(0, 2) as r:
                for d in range(KB):
                    mix_chunk(r, d)

            def product_block(b, s, k):
                hi, lo = split_hi[:, s, k * P:(k + 1) * P], split_lo[:, s, k * P:(k + 1) * P]
                for stat, mov, start, stop in ((hi, mat_hi, k == 0, False), (hi, mat_lo, False, False),
                                               (lo, mat_hi, False, k == KB - 1)):
                    for t in range(2):
                        last = nc.tensor.matmul(acc[:, b + t, :], stat, mov[:, k, t * HALF:(t + 1) * HALF],
                                                start=start, stop=stop)
                return last

            def mix_tile(j, p):
                pe.wait_ge(x_lo_made, j + 1)
                for k in range(KB):
                    pe.wait_ge(mix_lo_made, k + 1)
                    last = product_block(2 * p, p, k)
                last.then_inc(mixed, 1)

            pe.wait_ge(banks_free, 20)
            mix_tile(0, 0)
            mix_tile(1, 1)
            with pe.Fori(1, TILES // 2 - 1) as i:
                for p in range(2):
                    pe.wait_ge(mix_biased, 2 * i + p - 1)
                    mix_tile(2 * i + p, p)
            pe.wait_ge(mix_biased, TILES - 3)
            mix_tile(TILES - 2, 0)
            pe.wait_ge(eye_loaded, 16)

            def linear(sems, is_high):
                def turn(source, b, cols):
                    for n, c in enumerate(cols):
                        last = nc.tensor.transpose(acc[:, b + n // 4, (n % 4) * P:(n % 4 + 1) * P],
                                                   source(c), ident[:, :])
                    return last

                def turn_tokens(j, p, b):
                    pe.wait_ge(sems["tokens_copied"], j + 1)
                    turn(lambda k: stage[:, p, k * P:(k + 1) * P], b, range(KB)).then_inc(sems["tokens_turned"], 1)

                def turn_weights(k):
                    if k == 1:
                        pe.wait_ge(sems["tokens_lo"], 1)
                    elif k >= 2:
                        pe.wait_ge(sems["weights_lo"], k - 1)
                    turn(lambda ob: weights[:, ob, k * P:(k + 1) * P], 6 - 2 * (k % 2),
                         range(KB)).then_inc(sems["weights_turned"], 1)

                def linear_tile(j, p):
                    pe.wait_ge(sems["tokens_lo"], j + 1)
                    for t in range(2):
                        cols = slice(t * HALF, (t + 1) * HALF)
                        for k in range(KB):
                            hi, lo = split_hi[:, p, k * P:(k + 1) * P], split_lo[:, p, k * P:(k + 1) * P]
                            nc.tensor.matmul(acc[:, 2 * p + t, :], hi, mat_hi[:, k, cols], start=k == 0, stop=False)
                            nc.tensor.matmul(acc[:, 2 * p + t, :], hi, mat_lo[:, k, cols], start=False, stop=False)
                            last = nc.tensor.matmul(acc[:, 2 * p + t, :], lo, mat_hi[:, k, cols], start=False,
                                                    stop=k == KB - 1)
                        last.then_inc(sems["half_done"], 1)

                turn_tokens(0, 0, 4)
                pe.wait_ge(*((high_step, HIGH_STEPS * KB) if is_high else (decoded, DECODED_ALL)))
                turn_weights(0)
                if is_high:
                    turn_weights(1)
                else:
                    pe.wait_ge(x_lo_made, TILES)
                    pe.wait_ge(mix_biased, TILES - 2)
                    for k in range(KB):
                        if k == KB // 2:
                            turn_weights(1)
                        last = product_block(2, 1, k)
                    last.then_inc(mixed, 1)
                    pe.wait_ge(mix_biased, TILES)
                turn_tokens(1, 1, 2)
                for k in range(KB):
                    pe.wait_ge(sems["weights_lo"], k + 1)
                    if k + 2 < KB:
                        turn_weights(k + 2)
                    last = product_block(0, 0, k)
                last.then_inc(sems["half_done"], 2)
                turn_tokens(2, 0, 4)
                linear_tile(1, 1)
                turn_tokens(3, 1, 6)
                with pe.Fori(1, TILES // 2 - 1) as i:
                    for p in range(2):
                        pe.wait_ge(sems["summed"], 4 * i + 2 * p - 2)
                        linear_tile(2 * i + p, p)
                        turn_tokens(2 * i + p + 2, p, 4 + 2 * p)
                pe.wait_ge(sems["summed"], 2 * TILES - 6)
                linear_tile(TILES - 2, 0)
                if not is_high:
                    pe.wait_ge(any_made, 1)
                    nc.tensor.matmul(acc[0:1, 4, 0:1], any_high, one_col, start=True,
                                     stop=True).then_inc(flag_counted, 1)
                pe.wait_ge(sems["summed"], 2 * TILES - 4)
                linear_tile(TILES - 1, 1)

            linear(low, False)
            pe.wait_ge(flag_made, 1)
            wanted = nc.tensor.value_load(flag[0:1, 0:1], min_val=0, max_val=1)
            with nc.tensor.If(wanted > 0):
                linear(hi8, True)

        @block.scalar
        def _(act):
            act.wait_ge(consts_made, 2)
            nc.scalar.activation(stats[:, 0, 0:1], half_power, ACT.Gelu)
            def load_q(b):
                act.dma_start(q_low[:, :, :], qbits[bass.ds(b * P, P), 0:LOW_BITS, :]).then_inc(q_loaded, 16)

            def split_mix_rows(g):
                act.wait_ge(banks_free, 8 + 8 * (g // 4) + 4 + g % 4 + 1)
                nc.scalar.activation(mat_hi[:, g, :], weights[:, MASK_SLOT + g % 4, :],
                                     ACT.Copy).then_inc(mix_hi_made, 1)

            for c in range(CHUNKS):
                s, d = c % 2, c % KB
                act.wait_ge(w1_loaded[s], 16 * (c // 2 + 1))
                if c >= 2:
                    chunk_done(act, c - 2)
                nc.scalar.activation(split_hi[:, s, 0:HALF], w1_stage[:, s, :], ACT.Copy).then_inc(w1_hi_made, 1)
                if c == 0:
                    for t in range(2):
                        half = slice(t * HALF, (t + 1) * HALF)
                        act.wait_ge(w2_first_loaded[t], 16)
                        nc.scalar.activation(w2_hi[:, 0, half], stage[:, 0, half], ACT.Copy).then_inc(w2_hi_made, 1)
                    load_q(0)
                    act.dma_start(ident[:, :], eye).then_inc(eye_loaded, 16)
                elif c < KB:
                    act.wait_ge(w2_loaded[s], 16 * ((d + 1) // 2))
                    nc.scalar.activation(w2_hi[:, d, :], stage[:, STAGE_OF[s], :], ACT.Copy).then_inc(w2_hi_made, 1)
                if c == KB + 1:
                    for g in range(4):
                        split_mix_rows(g)
                steps = sum(n for at, n in EARLY.items() if at < c - 2)
                for b in blocks_started(steps, steps + EARLY.get(c - 2, 0)):
                    act.wait_ge(planes_made, b + 1)
                    load_q(b + 1)

            def split_x_cols(j, p):
                act.wait_ge(x_cols_loaded, 16 * j + 16)
                nc.scalar.activation(split_hi[:, p, :], stage[:, 0, :], ACT.Copy).then_inc(x_hi_made, 1)

            for p in range(2):
                chunk_done(act, CHUNKS - 2 + p)
                split_x_cols(p, p)
                split_mix_rows(4 + 2 * p)
                split_mix_rows(5 + 2 * p)
            steps = sum(n for at, n in EARLY.items() if at < CHUNKS - 2)
            for b in blocks_started(steps, EARLY_ALL):
                act.wait_ge(planes_made, b + 1)
                load_q(b + 1)

            def gelu(j):
                act.wait_ge(mix_biased, j + 1)
                nc.scalar.activation(x1[:, j, :], x1[:, j, :], ACT.Gelu).then_inc(gelu_done, 1)

            def squares1(j, p, more_rows):
                col = slice(p, p + 1)
                if more_rows:
                    act.wait_ge(residual_done, j + 1)
                    act.dma_start(stage[:, 2, :], x_rows[bass.ds((j + 1) * P, P), :]).then_inc(x_rows_loaded, 16)
                act.wait_ge(mean1, j + 1)
                if j:
                    act.wait_ge(energy_ready, j)
                nc.scalar.activation(junk[:, :], x1[:, j, :], ACT.Square, bias=neg_mean[:, col],
                                     accum_out=sqsum[:, col]).then_inc(squared1, 1)

            def scale1(j, p):
                col = slice(p, p + 1)
                act.wait_ge(shift1, j + 1)
                nc.scalar.activation(x1[:, j, :], x1[:, j, :], ACT.Identity, bias=shift[:, col],
                                     scale=rstd[:, col]).then_inc(x1_ready, 1)
                act.wait_ge(x1_ready, j + 1)
                nc.scalar.activation(junk[:, :], x1[:, j, :], ACT.Square,
                                     accum_out=energy[:, bass.ds(j, 1)]).then_inc(energy_ready, 1)

            for j in range(TILES - 2):
                act.wait_ge(mixed, j + 1)
                split_x_cols(j + 2, j % 2)
                gelu(j)
                if j:
                    scale1(j - 1, (j - 1) % 2)
                squares1(j, j % 2, True)
                for b in blocks_started(steps_by(j - 1), steps_by(j)):
                    if b + 1 < KB:
                        act.wait_ge(planes_made, b + 1)
                        load_q(b + 1)

            def linear(sems, is_high):
                def split_tokens(j, p, b):
                    act.wait_ge(sems["tokens_turned"], j + 1)
                    nc.scalar.activation(split_hi[:, p, :], banks(b), ACT.Copy).then_inc(sems["tokens_hi"], 1)

                def split_weights(k):
                    act.wait_ge(sems["weights_turned"], k + 1)
                    nc.scalar.activation(mat_hi[:, k, :], banks(6 - 2 * (k % 2)),
                                         ACT.Copy).then_inc(sems["weights_hi"], 1)

                if not is_high:
                    act.wait_ge(mixed, TILES - 1)
                    gelu(TILES - 2)
                    scale1(TILES - 3, 1)
                split_tokens(0, 0, 4)
                if not is_high:
                    squares1(TILES - 2, 0, True)
                    scale1(TILES - 2, 0)
                    act.wait_ge(mixed, TILES)
                split_weights(0)
                split_weights(1)
                split_tokens(1, 1, 2)
                split_weights(2)
                split_weights(3)
                if not is_high:
                    gelu(TILES - 1)
                for k in range(4, KB):
                    split_weights(k)
                if not is_high:
                    squares1(TILES - 1, 1, False)
                    scale1(TILES - 1, 1)

                def tile(j, p):
                    act.wait_ge(sems["half_done"], 2 * j + 2)
                    split_tokens(j + 2, p, 4 + 2 * p)

                with act.Fori(0, TILES // 2 - 1) as i:
                    for p in range(2):
                        tile(2 * i + p, p)

            linear(low, False)
            act.wait_ge(flag_made, 1)
            wanted = nc.scalar.value_load(flag[0:1, 0:1], min_val=0, max_val=1)
            with nc.scalar.If(wanted > 0):
                linear(hi8, True)

        @block.vector
        def _(dve):
            def make_planes(b, base):
                dve.wait_ge(q_loaded, 16 * b + 16)
                if b:
                    dve.wait_ge(decoded, base)
                q16 = q_low[:, :, :].bitcast(u16)
                for s in range(16):
                    last = nc.vector.tensor_scalar(planes[:, :, s * W16:(s + 1) * W16], q16, 1 << s, None,
                                                   ALU.bitwise_and)
                last.then_inc(planes_made, 1)
                dve.wait_ge(planes_made, b + 1)
                nc.vector.tensor_scalar(bit0_mask, plane0, 0.0, -1.0, ALU.is_gt, ALU.mult).then_inc(decoded, 1)

            def quarter(b, count, q, dest):
                if q in (0, 2):
                    dve.wait_ge(decoded, count)
                for n, to in ((0, dest), (1, leaf)):
                    if n == 1 and q in (1, 3):
                        dve.wait_ge(decoded, count)
                    leaf_no = 2 * q + n
                    last = nc.vector.tensor_scalar(to.bitcast(u32), bit0_mask.bitcast(u32),
                                                   lut_flip[:, b, leaf_no:leaf_no + 1],
                                                   lut[:, b, 2 * leaf_no:2 * leaf_no + 1].bitcast(u32),
                                                   ALU.bitwise_and, ALU.bitwise_xor)
                last.then_inc(decoded, 1)
                dve.wait_ge(decoded, count + 1)
                nc.vector.copy_predicated(dest, planes[:, 1, :], leaf).then_inc(decoded, 1)

            def merge(count, plane, dest, other):
                dve.wait_ge(decoded, count)
                nc.vector.copy_predicated(dest, planes[:, plane, :], other).then_inc(decoded, 1)

            def decode_step(n):
                b, step = divmod(n, STEPS)
                base, dest = DECODE_COUNT * b, weights[:, b, :]
                tmp, tmp2 = ((weights[:, b + 1, :], weights[:, b + 2, :]) if n < EARLY_ALL
                             else (x1[:, TILES - 2, :], x1[:, TILES - 1, :]))
                if step == 0:
                    make_planes(b, base)
                elif step == 1:
                    quarter(b, base + 1, 0, dest)
                elif step == 2:
                    quarter(b, base + 3, 1, tmp)
                elif step == 3:
                    merge(base + 5, 2, dest, tmp)
                elif step == 4:
                    quarter(b, base + 6, 2, tmp)
                elif step == 5:
                    quarter(b, base + 8, 3, tmp2)
                elif step == 6:
                    merge(base + 10, 2, tmp, tmp2)
                else:
                    merge(base + 11, 3, dest, tmp)

            def mask_mix_banks(r, t, sb_):
                dve.wait_ge(mask_loaded[sb_], 16 * (r + 1))
                dve.wait_ge(mix_bank_done, 8 * r + 4 * t + sb_ + 1)
                rows = weights[:, MASK_SLOT + sb_, t * HALF:(t + 1) * HALF]
                nc.vector.tensor_tensor(rows, acc[:, 4 * t + sb_, :], rows, ALU.mult).then_inc(banks_free, 1)

            def mix_lo(g):
                dve.wait_ge(mix_hi_made, g + 1)
                nc.vector.tensor_tensor(mat_lo[:, g, :], weights[:, MASK_SLOT + g % 4, :],
                                        mat_hi[:, g, :].bitcast(f32), ALU.subtract).then_inc(mix_lo_made, 1)

            def w2_lo_of(d, slot, cols):
                nc.vector.tensor_tensor(w2_lo[:, d, cols], stage[:, slot, cols], w2_hi[:, d, cols].bitcast(f32),
                                        ALU.subtract).then_inc(w2_lo_made, 1)

            def x_lo(j, p):
                dve.wait_ge(x_hi_made, j + 1)
                nc.vector.tensor_tensor(split_lo[:, p, :], stage[:, 0, :], split_hi[:, p, :].bitcast(f32),
                                        ALU.subtract).then_inc(x_lo_made, 1)

            step = 0
            for c in range(CHUNKS):
                s, d = c % 2, c % KB
                dve.wait_ge(w1_hi_made, c + 1)
                nc.vector.tensor_tensor(split_lo[:, s, 0:HALF], w1_stage[:, s, :],
                                        split_hi[:, s, 0:HALF].bitcast(f32), ALU.subtract).then_inc(w1_lo_made, 1)
                if c == 0:
                    for t in range(2):
                        dve.wait_ge(w2_hi_made, t + 1)
                        w2_lo_of(0, 0, slice(t * HALF, (t + 1) * HALF))
                elif c < KB:
                    dve.wait_ge(w2_hi_made, d + 2)
                    w2_lo_of(d, STAGE_OF[s], slice(0, D))
                if c == 1:
                    dve.wait_ge(lut_loaded, 16)
                    pairs = lut[:, :, :].bitcast(u32).rearrange("p b (j t) -> p b j t", t=2)
                    nc.vector.tensor_tensor(lut_flip[:, :, :], pairs[:, :, :, 0], pairs[:, :, :, 1],
                                            ALU.bitwise_xor).then_inc(flips_made, 1)
                    dve.wait_ge(flips_made, 1)
                if c == KB:
                    for t in range(2):
                        for sb_ in range(4):
                            mask_mix_banks(0, t, sb_)
                if c == KB + 1:
                    for g in range(4):
                        mix_lo(g)
                for _ in range(EARLY.get(c, 0)):
                    decode_step(step)
                    step += 1
            x_lo(0, 0)
            for sb_ in range(4):
                mask_mix_banks(1, 0, sb_)
            for sb_ in range(4):
                mask_mix_banks(1, 1, sb_)
                if sb_ >= 1:
                    mix_lo(3 + sb_)
            mix_lo(7)
            x_lo(1, 1)

            def bias_mix(j, p):
                dve.wait_ge(mixed, j + 1)
                dve.wait_ge(b2_loaded, 16)
                nc.vector.tensor_tensor(x1[:, j, :], banks(2 * p), row_bc[:, :], ALU.add).then_inc(mix_biased, 1)

            def residual(j, p):
                dve.wait_ge(gelu_done, j + 1)
                dve.wait_ge(x_rows_loaded, 16 * j + 16)
                nc.vector.scalar_tensor_tensor(x1[:, j, :], x1[:, j, :], 1.0, stage[:, 2, :], ALU.mult, ALU.add,
                                               accum_out=zsum[:, p:p + 1]).then_inc(residual_done, 1)

            for j in range(TILES - 2):
                bias_mix(j, j % 2)
                for n in range(steps_by(j - 1), steps_by(j)):
                    if n == steps_by(j - 1) + 1:
                        residual(j, j % 2)
                    decode_step(n)

            def linear(sems, is_high):
                def copy_tokens(j, p):
                    if not is_high:
                        dve.wait_ge(x1_ready, j + 1)
                    nc.vector.tensor_copy(stage[:, p, :].rearrange("p (s w) -> p s w", s=16),
                                          permuted(x1[:, j, :])).then_inc(sems["tokens_copied"], 1)

                def tokens_lo(j, p, b):
                    dve.wait_ge(sems["tokens_hi"], j + 1)
                    nc.vector.tensor_tensor(split_lo[:, p, :], banks(b), split_hi[:, p, :].bitcast(f32),
                                            ALU.subtract).then_inc(sems["tokens_lo"], 1)

                def weights_lo(k):
                    dve.wait_ge(sems["weights_hi"], k + 1)
                    nc.vector.tensor_tensor(mat_lo[:, k, :], banks(6 - 2 * (k % 2)), mat_hi[:, k, :].bitcast(f32),
                                            ALU.subtract).then_inc(sems["weights_lo"], 1)

                def add_bias(j, s):
                    nc.vector.tensor_tensor(weights[:, s, :], x1[:, j, :], row_bc[:, :],
                                            ALU.add).then_inc(sems["biased"], 1)

                if not is_high:
                    dve.wait_ge(decoded, DECODED_ALL)
                    bias_mix(TILES - 2, 0)
                    dve.wait_ge(x_lo_made, TILES)
                copy_tokens(0, 0)
                copy_tokens(1, 1)
                tokens_lo(0, 0, 4)
                if not is_high:
                    residual(TILES - 2, 0)
                    bias_mix(TILES - 1, 1)
                weights_lo(0)
                weights_lo(1)
                tokens_lo(1, 1, 2)
                for k in range(2, 5):
                    weights_lo(k)
                if not is_high:
                    residual(TILES - 1, 1)
                for k in range(5, KB):
                    weights_lo(k)
                dve.wait_ge(sems["tokens_turned"], 1)
                copy_tokens(2, 0)
                dve.wait_ge(sems["weights_turned"], KB)
                dve.wait_ge(bias_loaded, 16)
                if not is_high:
                    dve.wait_ge(x1_ready, 2)
                add_bias(0, 0)
                add_bias(1, 1)

                def tile(j, s, split_next, copy_next, stored):
                    p = s % 2
                    for t in range(2):
                        half = slice(t * HALF, (t + 1) * HALF)
                        dve.wait_ge(sems["half_done"], 2 * j + t + 1)
                        if t == 0:
                            dve.wait_ge(sems["biased"], j + 1)
                        nc.vector.tensor_tensor(weights[:, s, half], acc[:, 2 * p + t, :], weights[:, s, half],
                                                ALU.add).then_inc(sems["summed"], 1)
                        if t == 0 and copy_next:
                            dve.wait_ge(sems["tokens_turned"], j + 2)
                            copy_tokens(j + 3, 1 - p)
                        dve.wait_ge(sems["summed"], 2 * j + t + 1)
                        nc.vector.bn_stats(halves[:, t, :], weights[:, s, half]).then_inc(sems["half_stats"], 1)
                    dve.wait_ge(sems["half_stats"], 2 * j + 2)
                    if split_next:
                        tokens_lo(j + 2, p, 4 + 2 * p)
                    nc.vector.bn_aggr(moments[:, p, :], halves[:, :, :].rearrange("p a b -> p (a b)")).then_inc(
                        sems["tile_stats"], 1)
                    if split_next:
                        if stored is not None:
                            dve.wait_ge(sems["stored"][(s + 2) % RING], stored)
                        add_bias(j + 2, (s + 2) % RING)
                    dve.wait_ge(sems["rstd"], j + 1)
                    for t in range(2):
                        rows = weights[:, s, t * HALF:(t + 1) * HALF]
                        nc.vector.tensor_scalar(rows, rows, moments[:, p, 0:1], rstd[:, p:p + 1],
                                                ALU.subtract, ALU.mult).then_inc(sems["normed"], 1)
                    if is_high:
                        rows = weights[:, s, :].bitcast(i32)
                        kept = stage[:, 2, :].bitcast(i32)
                        dve.wait_ge(sems["normed"], 2 * j + 2)
                        dve.wait_ge(sems["low_rows_loaded"], 16 * j + 16)
                        nc.vector.tensor_tensor(rows, rows, kept, ALU.bitwise_xor).then_inc(sems["compared"], 1)
                        dve.wait_ge(sems["compared"], j + 1)
                        nc.vector.scalar_tensor_tensor(kept, rows, high_bits[:, bass.ds(j, 1)], kept,
                                                       ALU.bitwise_and, ALU.bitwise_xor).then_inc(sems["blended"], 1)

                for s in range(RING):
                    tile(s, s, True, True, 32 if s >= 2 else None)
                with dve.Fori(1, TILES // RING - 1) as g:
                    for s in range(RING):
                        tile(RING * g + s, s, True, True, 32 * g + (32 if s >= 2 else 0))
                for s in range(RING):
                    tile(TILES - RING + s, s, s < 2, s < 1, 32 * (TILES // RING - 1))
                    if s == 1 and not is_high:
                        decide()

            def decide():
                dve.wait_ge(high_made, 1)
                nc.vector.tensor_scalar(high_bits[:, :], high, -1.0, None, ALU.mult)
                nc.vector.reduce_max(any_high, high, mybir.AxisListType.X).then_inc(any_made, 1)
                dve.wait_ge(flag_counted, 1)
                nc.vector.tensor_scalar(flag[0:1, 0:1], acc[0:1, 4, 0:1], 0.0, None, ALU.is_gt).then_inc(flag_made, 1)

            linear(low, False)
            dve.wait_ge(flag_made, 1)
            wanted = nc.vector.value_load(flag[0:1, 0:1], min_val=0, max_val=1)
            with nc.vector.If(wanted > 0):
                for s in range(RING):
                    dve.wait_ge(low["stored"][s], 32 * (TILES // RING))
                q_high = stage[:, 2, 0:HIGH_BITS * WORDS].bitcast(u16).rearrange("p (n w) -> p n w", n=HIGH_BITS)
                table = stage[:, 2, 256:512]
                code, bits, hit = stage[:, 1, :], planes[:, 1, :], stage[:, 0, :].bitcast(i32)
                with dve.Fori(0, KB) as b:
                    base = HIGH_STEPS * b
                    dve.wait_ge(high_bits_loaded, 32 * b + 32)
                    row = weights[:, b, :].bitcast(i32)
                    nc.vector.tensor_scalar(row, row, 0, None, ALU.bitwise_and).then_inc(high_step, 1)
                    dve.wait_ge(high_step, base + 1)
                    nc.vector.tensor_scalar(code.bitcast(i32), code.bitcast(i32), 0, None,
                                            ALU.bitwise_and).then_inc(high_step, 1)
                    for n in range(HIGH_BITS):
                        dve.wait_ge(high_step, base + 2 * n + 2)
                        for s in range(16):
                            last = nc.vector.tensor_scalar(bits[:, s * W16:(s + 1) * W16],
                                                           q_high[:, HIGH_BITS - 1 - n, :], s, 1,
                                                           ALU.logical_shift_right, ALU.bitwise_and)
                        last.then_inc(high_step, 1)
                        dve.wait_ge(high_step, base + 2 * n + 3)
                        nc.vector.scalar_tensor_tensor(code, code, 2.0, bits, ALU.mult,
                                                       ALU.add).then_inc(high_step, 1)
                    with dve.Fori(0, 2 ** HIGH_BITS) as k:
                        dve.wait_ge(high_step, base + 2 + 2 * HIGH_BITS + 2 * k)
                        nc.vector.tensor_scalar(hit, code, 0.0, -1.0, ALU.is_equal, ALU.mult).then_inc(high_step, 1)
                        dve.wait_ge(high_step, base + 3 + 2 * HIGH_BITS + 2 * k)
                        nc.vector.scalar_tensor_tensor(row, hit, table[:, bass.ds(k, 1)].bitcast(i32), row,
                                                       ALU.bitwise_and, ALU.bitwise_or)
                        nc.vector.tensor_scalar(code, code, -1.0, None, ALU.add).then_inc(high_step, 1)
                dve.wait_ge(high_step, HIGH_STEPS * KB)
                linear(hi8, True)

        @block.gpsimd
        def _(pool):
            nc.gpsimd.memset(junk[:, :], 1.0).then_inc(warm_made, 1)
            nc.gpsimd.memset(half_powers, 0.5).then_inc(consts_made, 1)
            nc.gpsimd.memset(half_power, 0.5).then_inc(consts_made, 1)
            nc.gpsimd.memset(minus_half_power, -0.5).then_inc(consts_made, 1)
            nc.gpsimd.memset(one_col, 1.0).then_inc(consts_made, 1)
            nc.gpsimd.memset(inv_d, 1.0 / D).then_inc(consts_made, 1)
            nc.gpsimd.memset(neg_inv_d, -1.0 / D).then_inc(consts_made, 1)
            nc.gpsimd.memset(eps_col, EPS).then_inc(consts_made, 1)
            nc.gpsimd.memset(zero_col, 0.0).then_inc(banks_free, 8)
            pool.wait_ge(consts_made, 7)

            def statistics1(j, p):
                col = slice(p, p + 1)
                pool.wait_ge(residual_done, j + 1)
                nc.gpsimd.tensor_tensor(neg_mean[:, col], zsum[:, col], neg_inv_d, ALU.mult).then_inc(mean1, 1)
                pool.wait_ge(squared1, j + 1)
                nc.gpsimd.tensor_tensor(var[:, col], sqsum[:, col], inv_d, ALU.mult).then_inc(var1, 1)
                pool.wait_ge(var1, 2 * j + 1)
                nc.gpsimd.tensor_tensor(var[:, col], var[:, col], eps_col, ALU.add).then_inc(var1, 1)
                pool.wait_ge(var1, 2 * j + 2)
                nc.gpsimd.tensor_tensor(rstd[:, col], var[:, col], minus_half_power, ALU.pow).then_inc(rstd1, 1)
                pool.wait_ge(rstd1, j + 1)
                nc.gpsimd.tensor_tensor(shift[:, col], neg_mean[:, col], rstd[:, col], ALU.mult).then_inc(shift1, 1)

            with pool.Fori(0, TILES // 2 - 1) as i:
                for p in range(2):
                    j = 2 * i + p
                    pool.wait_ge(x_hi_made, j + 3)
                    nc.gpsimd.tensor_tensor(split_lo[:, p, :], stage[:, 0, :], split_hi[:, p, :].bitcast(f32),
                                            ALU.subtract).then_inc(x_lo_made, 1)
                    statistics1(j, p)
            statistics1(TILES - 2, 0)
            statistics1(TILES - 1, 1)

            pool.wait_ge(energy_ready, TILES)
            nc.gpsimd.tensor_tensor(norm, energy[:, :], half_powers, ALU.pow).then_inc(norm_made, 1)
            pool.wait_ge(norm_made, 1)
            nc.gpsimd.tensor_scalar(norm, norm, LIN_SLOPE, LIN_INTER, ALU.mult, ALU.add).then_inc(norm_made, 1)
            pool.wait_ge(norm_made, 2)
            nc.gpsimd.tensor_scalar(high, norm, EST_T, None, ALU.is_gt).then_inc(high_made, 1)

            def linear(sems):
                with pool.Fori(0, TILES // 2) as i:
                    for p in range(2):
                        j, col = 2 * i + p, slice(p, p + 1)
                        pool.wait_ge(sems["tile_stats"], j + 1)
                        nc.gpsimd.tensor_tensor(var[:, col], moments[:, p, 1:2], eps_col,
                                                ALU.add).then_inc(sems["variance"], 1)
                        pool.wait_ge(sems["variance"], j + 1)
                        nc.gpsimd.tensor_tensor(rstd[:, col], var[:, col], minus_half_power,
                                                ALU.pow).then_inc(sems["rstd"], 1)

            linear(low)
            pool.wait_ge(flag_made, 1)
            wanted = nc.gpsimd.value_load(flag[0:1, 0:1], min_val=0, max_val=1)
            with nc.gpsimd.If(wanted > 0):
                linear(hi8)


def kernel(L0_attn_x, L0_attn_w1, L0_attn_w2, L0_attn_b2, L0_attn_sparse_mask, L0_ffn_qweight, L0_ffn_lut4,
           L0_ffn_lut8, L0_ffn_bias):
    import concourse.bacc as bacc
    from concourse.bass_utils import run_bass_kernel_spmd as run

    x = np.asarray(L0_attn_x)
    batch, seq, d = x.shape
    tokens = batch * seq
    rows = np.ascontiguousarray(x.reshape(tokens, d))
    cols = np.ascontiguousarray(rows.reshape(tokens // P, P, d // P, P).transpose(0, 3, 2, 1)).reshape(
        tokens // P, P, d)
    arrays = {
        "x_rows": rows,
        "x_cols": cols,
        "w1": np.ascontiguousarray(L0_attn_w1),
        "w2_cols": np.ascontiguousarray(np.asarray(L0_attn_w2).T),
        "b2": np.ascontiguousarray(L0_attn_b2).reshape(1, d),
        "mask": np.ascontiguousarray(L0_attn_sparse_mask),
        "qbits": np.ascontiguousarray(np.asarray(L0_ffn_qweight).transpose(1, 0, 2)),
        "lut4": np.ascontiguousarray(np.asarray(L0_ffn_lut4).reshape(d // P, P, -1).transpose(1, 0, 2)),
        "lut8": np.ascontiguousarray(L0_ffn_lut8),
        "bias": np.ascontiguousarray(L0_ffn_bias).reshape(1, d),
        "eye": np.eye(P, dtype=np.float32),
    }
    nc = bacc.Bacc("TRN2", target_bir_lowering=False, num_devices=1)
    args = [nc.dram_tensor(f"in_{name}", a.shape, mybir.dt.from_np(a.dtype), kind="ExternalInput").ap()
            for name, a in arrays.items()]
    out = nc.dram_tensor("out_rows", (tokens, d), mybir.dt.float32, kind="ExternalOutput").ap()
    post_ln_block(nc, *args, out)
    result = run(nc, [{f"in_{name}": a for name, a in arrays.items()}], core_ids=[0])
    return result.results[0]["out_rows"].reshape(batch, seq, d)
```

```python
import numpy as np
from contextlib import ExitStack

import concourse.bass as bass
from concourse import mybir

P = 128
EPS = 1e-5
EST_T = 64.0
LIN_SLOPE, LIN_INTER = 1.0, 0.0


PASS_SIGNALS = ("blocks_turned", "tokens_hi", "tokens_lo", "rows_turned", "rows_moved", "weights_hi",
                "weights_lo", "half_done", "biased", "summed", "half_stats", "tile_stats", "variance", "rstd",
                "normed", "low_rows_loaded", "compared", "blended")


def pass_semaphores(new, prefix):
    sems = {name: new(f"{prefix}_{name}") for name in PASS_SIGNALS}
    sems["stored"] = [new(f"{prefix}_stored{s}") for s in range(4)]
    sems["tokens_turned"] = [new(f"{prefix}_turned{p}") for p in range(2)]
    return sems


def post_ln_block(nc, x_rows, x_cols, w1, w2_cols, b2, mask, qbits, lut4, lut8, bias, out):
    f32, f32r, bf16 = mybir.dt.float32, mybir.dt.float32r, mybir.dt.bfloat16
    i32, u32, u16 = mybir.dt.int32, mybir.dt.uint32, mybir.dt.uint16
    ALU, ACT = mybir.AluOpType, mybir.ActivationFunctionType

    TOKENS, D = x_rows.shape
    TILES = TOKENS // P
    KB = D // P
    HALF = D // 2
    WORDS = D // 32
    W16 = 2 * WORDS
    LOW_BITS, HIGH_BITS = 4, 8
    RING = 4
    WARM_UP = 9
    MASK_SLOT = KB // 2
    CHUNKS = 2 * KB

    ctx = ExitStack()
    with ctx:
        def sb(name, shape, dt):
            return ctx.enter_context(nc.sbuf_tensor(name, shape, dt))

        def sem(name):
            return ctx.enter_context(nc.semaphore(name))

        mat_hi = sb("mat_hi", [P, KB, D], f32r)
        mat_lo = sb("mat_lo", [P, KB, D], f32r)
        weights = sb("weights", [P, KB, D], f32)
        stage = sb("stage", [P, 3, D], f32)
        split_hi = sb("split_hi", [P, 2, D], f32r)
        split_lo = sb("split_lo", [P, 2, D], f32r)
        row_bc = sb("row_bc", [P, D], f32)
        decode = sb("decode", [P, 2 * D + 3 * D], u16)
        lut = sb("lut", [P, KB, 16], f32)
        lut_flip = sb("lut_flip", [P, KB, 8], u32)
        q_low = sb("q_low", [P, LOW_BITS, WORDS], i32)
        junk = sb("junk", [P, D], bf16)
        halves = sb("halves", [P, 2, 6], f32)
        moments = sb("moments", [P, 2, 2], f32)
        stats = sb("stats", [P, 6, 2], f32)
        energy = sb("energy", [P, TILES], f32)
        gate = sb("gate", [P, 3 * TILES + 8], f32)
        high_bits = sb("high_bits", [P, TILES], i32)
        flag = sb("flag", [1, 1], i32)
        with ExitStack() as early:
            w2_hi = early.enter_context(nc.sbuf_tensor("w2_hi", [P, KB, D], f32r))
            w2_lo = early.enter_context(nc.sbuf_tensor("w2_lo", [P, KB, D], f32r))
        x1 = sb("x1", [P, TILES, D], f32)
        acc = ctx.enter_context(nc.psum_tensor("acc", [P, 8, HALF], f32))

        leaf = decode[:, 0:2 * D].bitcast(f32)
        planes = decode[:, D:D + LOW_BITS * D].rearrange("p (n c) -> p n c", n=LOW_BITS)
        plane0 = planes[:, 0, :]
        bit0_mask = stage[:, 1, :].bitcast(i32)
        w1_stage = row_bc[:, :].rearrange("p (s c) -> p s c", s=2)
        STAGE_OF = (0, 2)
        zsum, neg_mean, sqsum, var, rstd, shift = (stats[:, n, :] for n in range(6))
        half_power = gate[:, 3 * TILES:3 * TILES + 1]
        minus_half_power = gate[:, 3 * TILES + 1:3 * TILES + 2]
        any_high = gate[:, 3 * TILES + 2:3 * TILES + 3]
        one_col = gate[:, 3 * TILES + 3:3 * TILES + 4]
        inv_d, neg_inv_d, eps_col, zero_col = (gate[:, n:n + 1] for n in range(3 * TILES + 4, 3 * TILES + 8))
        norm, half_powers, high = (gate[:, n * TILES:(n + 1) * TILES] for n in range(3))

        def banks(b):
            return acc[:, b:b + 2, :].rearrange("p b n -> p (b n)")

        MOVES = 4
        moved = decode[:, 0:4 * D].bitcast(f32).rearrange("p (s c) -> p s c", s=2)

        def token_blocks(row):
            return row.rearrange("p (n f) -> p f n", n=2)

        def weight_blocks(row):
            return row.rearrange("p (i m) -> p m i", m=32)

        def move_blocks(queue, dest, source, moves_done):
            for a in range(MOVES):
                queue.dma_start(dest[:, a * D // 4:(a + 1) * D // 4],
                                source[32 * a:32 * a + 32, :]).then_inc(moves_done, 16)

        def move_tokens(queue, sems, p):
            move_blocks(queue, moved[:, p, :], stage[:, p, :], sems["tokens_turned"][p])

        def turned_weights(k):
            return weights[:, :, :].rearrange("p b d -> p (b d)").rearrange("p (g k c) -> p k g c", k=KB,
                                                                            c=32)[:, k, :, :]

        def by_group(row):
            return row.rearrange("p (g c) -> p g c", c=32)

        def features_by_token(row):
            return row.rearrange("p (a k c) -> p k a c", a=4, c=32)

        def turned(row):
            return row.rearrange("p (k a c) -> p k a c", a=4, c=32)

        w1_loaded = [sem(f"w1_loaded{s}") for s in range(2)]
        w2_first_loaded = [sem(f"w2_first_loaded{t}") for t in range(2)]
        w2_loaded = [sem(f"w2_loaded{s}") for s in range(2)]
        mask_loaded = [sem(f"mask_loaded{s}") for s in range(4)]
        lut_loaded, q_loaded = sem("lut_loaded"), sem("q_loaded")
        b2_loaded, bias_loaded = sem("b2_loaded"), sem("bias_loaded")
        x_cols_loaded, x_rows_loaded = sem("x_cols_loaded"), sem("x_rows_loaded")
        w1_hi_made, w1_lo_made, w2_hi_made, w2_lo_made = (sem(n) for n in ("w1_hi", "w1_lo", "w2_hi_m", "w2_lo_m"))
        chunk_used, mix_bank_done = sem("chunk_used"), sem("mix_bank_done")
        banks_free = sem("banks_free")
        mix_hi_made, mix_lo_made = sem("mix_hi_made"), sem("mix_lo_made")
        flips_made, planes_made, decoded = sem("flips_made"), sem("planes_made"), sem("decoded")
        x_hi_made, x_lo_made, mixed = sem("x_hi_made"), sem("x_lo_made"), sem("mixed")
        mix_block_used = sem("mix_block_used")
        mix_biased, gelu_done, residual_done = sem("mix_biased"), sem("gelu_done"), sem("residual_done")
        mean1, squared1, var1, rstd1, shift1 = (sem(n) for n in ("mean1", "squared1", "var1", "rstd1", "shift1"))
        x1_ready, energy_ready = sem("x1_ready"), sem("energy_ready")
        warm_made = sem("warm_made")
        consts_made, norm_made, high_made = sem("consts_made"), sem("norm_made"), sem("high_made")
        any_made, flag_counted, flag_made = sem("any_made"), sem("flag_counted"), sem("flag_made")
        high_bits_loaded, high_step = sem("high_bits_loaded"), sem("high_step")
        low = pass_semaphores(sem, "low")
        hi8 = pass_semaphores(sem, "high")

        DECODE_COUNT = 12
        DECODED_ALL = DECODE_COUNT * KB
        LENGTHS = (5, 5, 5, 2, 5, 5, 2, 2, 2)
        STEPS = len(LENGTHS)
        EARLY = {1: 1, 2: 1, 3: 1, 4: 2, 5: 1, 6: 2, 7: 1, 9: 2, 10: 1, 11: 2, 12: 2, 13: 3, 14: 2, 15: 1}
        EARLY_ALL = sum(EARLY.values())
        LATE_TILES = TILES - 2
        LATE_LENGTH = sum(LENGTHS[n % STEPS] for n in range(EARLY_ALL, STEPS * KB))

        def steps_by(j):
            n, length = EARLY_ALL, 0
            while n < STEPS * KB and length * LATE_TILES < LATE_LENGTH * (j + 1):
                length += LENGTHS[n % STEPS]
                n += 1
            return n

        def blocks_turned_in(first, end):
            return [n // STEPS for n in range(first, end) if n % STEPS == STEPS - 1]

        def turn_slot(b):
            if STEPS * (b + 1) > EARLY_ALL:
                return x1[:, TILES - 1, :]
            return (weights if b == 0 else x1)[:, 2, :]

        def blocks_started(first, end):
            return [n // STEPS for n in range(first, end) if n % STEPS == 0]

        HIGH_STEPS = 2 + 2 * HIGH_BITS + 2 * 2 ** HIGH_BITS

        def chunk_done(eng, c):
            r, d = divmod(c, KB)
            if d < KB - 1:
                eng.wait_ge(chunk_used, (KB - 1) * r + d + 1)
            else:
                eng.wait_ge(mix_bank_done, 8 * (r + 1))

        block = ctx.enter_context(nc.Block())

        @block.sync
        def _(sp):
            def load_x_cols(j):
                sp.dma_start(stage[:, 0, :], x_cols[j]).then_inc(x_cols_loaded, 16)

            def load_mask(g):
                if g >= 4:
                    sp.wait_ge(mix_lo_made, g - 3)
                sp.dma_start(weights[:, MASK_SLOT + g % 4, :],
                             mask[g * P:(g + 1) * P, :]).then_inc(mask_loaded[g % 4], 16)

            def move_weights(blocks):
                for b in blocks:
                    sp.wait_ge(low["rows_turned"], b + 1)
                    move_blocks(sp, weights[:, b, :], turn_slot(b), low["rows_moved"])

            for c in range(CHUNKS):
                r, d = divmod(c, KB)
                if c >= 2:
                    sp.wait_ge(w1_lo_made, c - 1)
                sp.dma_start(w1_stage[:, c % 2, :],
                             w1[d * P:(d + 1) * P, r * HALF:(r + 1) * HALF]).then_inc(w1_loaded[c % 2], 16)
                if c == 0:
                    for t in range(2):
                        half = slice(t * HALF, (t + 1) * HALF)
                        sp.dma_start(stage[:, 0, half], w2_cols[0:P, half]).then_inc(w2_first_loaded[t], 16)
                elif c < KB:
                    if c >= 2:
                        sp.wait_ge(w2_lo_made, c)
                    sp.dma_start(stage[:, STAGE_OF[d % 2], :],
                                 w2_cols[d * P:(d + 1) * P, :]).then_inc(w2_loaded[d % 2], 16)
                if c == 0:
                    sp.dma_start(lut[:, :, :], lut4).then_inc(lut_loaded, 16)
                if c in (3, 4, 5, 6):
                    load_mask(c - 3)
                if c == 11:
                    sp.wait_ge(w2_lo_made, KB + 1)
                    load_x_cols(0)
                    sp.dma_start(stage[:, 2, :], x_rows[0:P, :]).then_inc(x_rows_loaded, 16)
                if c in (12, 13, 14, 15):
                    load_mask(c - 8)
                steps = sum(n for at, n in EARLY.items() if at < c - 2)
                move_weights(blocks_turned_in(steps, steps + EARLY.get(c - 2, 0)))
            sp.wait_ge(w1_lo_made, CHUNKS)
            sp.dma_start(row_bc[:, :], b2.broadcast_to([P, D])).then_inc(b2_loaded, 16)
            steps = sum(n for at, n in EARLY.items() if at < CHUNKS - 2)
            move_weights(blocks_turned_in(steps, EARLY_ALL))
            for j in range(1, TILES):
                sp.wait_ge(x_lo_made, j)
                load_x_cols(j)
                if j >= 3:
                    move_weights(blocks_turned_in(steps_by(j - 4), steps_by(j - 3)))
            move_weights(blocks_turned_in(steps_by(TILES - 4), STEPS * KB))

            def move_first_blocks(sems):
                for p in range(2):
                    sp.wait_ge(sems["blocks_turned"], p + 1)
                    move_tokens(sp, sems, p)

            move_first_blocks(low)
            sp.wait_ge(mix_biased, TILES)
            sp.dma_start(row_bc[:, :], bias.broadcast_to([P, D])).then_inc(bias_loaded, 16)

            with sp.Fori(0, TILES // RING) as g:
                for s in range(RING):
                    for t in range(2):
                        j, half = RING * g + s, slice(t * HALF, (t + 1) * HALF)
                        sp.wait_ge(low["normed"], 2 * j + t + 1)
                        sp.dma_start(out[bass.ds(j * P, P), half], weights[:, s, half]).then_inc(low["stored"][s], 16)
            sp.wait_ge(flag_made, 1)
            wanted = nc.sync.value_load(flag[0:1, 0:1], min_val=0, max_val=1)
            for s in range(RING):
                sp.wait_ge(low["stored"][s], 32 * (TILES // RING))
            with nc.sync.If(wanted > 0):
                for b in range(KB):
                    sp.dma_start(stage[:, 2, 0:HIGH_BITS * WORDS].bitcast(i32),
                                 qbits[bass.ds(b * P, P), :, :].rearrange("p n w -> p (n w)")).then_inc(
                                     high_bits_loaded, 16)
                    sp.dma_start(stage[:, 2, 256:512], lut8[bass.ds(b * P, P), :]).then_inc(high_bits_loaded, 16)
                    sp.wait_ge(high_step, HIGH_STEPS * (b + 1))
                for b in range(KB):
                    sp.wait_ge(hi8["rows_turned"], b + 1)
                    move_blocks(sp, weights[:, b, :], stage[:, 0, :], hi8["rows_moved"])
                move_first_blocks(hi8)
                for g in range(TILES // RING):
                    for s in range(RING):
                        j = RING * g + s
                        sp.dma_start(stage[:, 2, :], out[bass.ds(j * P, P), :]).then_inc(hi8["low_rows_loaded"], 16)
                        sp.wait_ge(hi8["blended"], j + 1)
                        sp.dma_start(out[bass.ds(j * P, P), :], stage[:, 2, :]).then_inc(hi8["stored"][s], 32)
                        sp.wait_ge(hi8["stored"][s], 32 * g + 32)

        @block.tensor
        def _(pe):
            pe.wait_ge(warm_made, 1)
            for _ in range(WARM_UP):
                nc.tensor.matmul(acc[:, 7, :], junk[:, 0:P], junk[:, 0:HALF], start=True, stop=True)

            def mix_chunk(r, d):
                s, start, stop = d % 2, d == 0, d == KB - 1
                for t in range(2):
                    cols = slice(t * HALF, (t + 1) * HALF)
                    if start and t == 0:
                        pe.wait_ge(w1_hi_made, KB * r + 1)
                        pe.wait_ge(w2_hi_made, 1)
                        for sb_ in range(4):
                            pe.wait_ge(banks_free, 8 * r + sb_ + 1)
                            nc.tensor.matmul(acc[:, sb_, :], split_hi[:, s, sb_ * P:(sb_ + 1) * P], w2_hi[:, 0, cols],
                                             start=True, stop=False)
                    pe.wait_ge(w1_lo_made, KB * r + d + 1)
                    pe.wait_ge(w2_lo_made, d + 2 if d else t + 1)
                    for sb_ in range(4):
                        bank = acc[:, 4 * t + sb_, :]
                        rows = slice(sb_ * P, (sb_ + 1) * P)
                        hi, lo = split_hi[:, s, rows], split_lo[:, s, rows]
                        if start and t == 1:
                            pe.wait_ge(banks_free, 8 * r + 4 + sb_ + 1)
                        if not start or t == 1:
                            nc.tensor.matmul(bank, hi, w2_hi[:, d, cols], start=start, stop=False)
                        nc.tensor.matmul(bank, hi, w2_lo[:, d, cols], start=False, stop=False)
                        last = nc.tensor.matmul(bank, lo, w2_hi[:, d, cols], start=False, stop=stop)
                        if stop:
                            last.then_inc(mix_bank_done, 1)
                if not stop:
                    last.then_inc(chunk_used, 1)

            with pe.Fori(0, 2) as r:
                for d in range(KB):
                    mix_chunk(r, d)

            def product_block(b, s, k):
                hi, lo = split_hi[:, s, k * P:(k + 1) * P], split_lo[:, s, k * P:(k + 1) * P]
                for stat, mov, start, stop in ((hi, mat_hi, k == 0, False), (hi, mat_lo, False, False),
                                               (lo, mat_hi, False, k == KB - 1)):
                    for t in range(2):
                        last = nc.tensor.matmul(acc[:, b + t, :], stat, mov[:, k, t * HALF:(t + 1) * HALF],
                                                start=start, stop=stop)
                return last

            def mix_tile(j, p):
                pe.wait_ge(x_lo_made, j + 1)
                for k in range(KB):
                    pe.wait_ge(mix_lo_made, k + 1)
                    last = product_block(2 * p, p, k)
                last.then_inc(mixed, 1)

            pe.wait_ge(banks_free, 20)
            mix_tile(0, 0)
            mix_tile(1, 1)
            with pe.Fori(1, TILES // 2 - 1) as i:
                for p in range(2):
                    pe.wait_ge(mix_biased, 2 * i + p - 1)
                    mix_tile(2 * i + p, p)
            pe.wait_ge(mix_biased, TILES - 3)
            mix_tile(TILES - 2, 0)

            def linear(sems, is_high):
                def linear_tile(j, p):
                    pe.wait_ge(sems["tokens_lo"], j + 1)
                    for t in range(2):
                        cols = slice(t * HALF, (t + 1) * HALF)
                        for k in range(KB):
                            hi, lo = split_hi[:, p, k * P:(k + 1) * P], split_lo[:, p, k * P:(k + 1) * P]
                            nc.tensor.matmul(acc[:, 2 * p + t, :], hi, mat_hi[:, k, cols], start=k == 0, stop=False)
                            nc.tensor.matmul(acc[:, 2 * p + t, :], hi, mat_lo[:, k, cols], start=False, stop=False)
                            last = nc.tensor.matmul(acc[:, 2 * p + t, :], lo, mat_hi[:, k, cols], start=False,
                                                    stop=k == KB - 1)
                        last.then_inc(sems["half_done"], 1)

                if not is_high:
                    pe.wait_ge(x_lo_made, TILES)
                    pe.wait_ge(mix_biased, TILES - 2)
                    for k in range(KB):
                        product_block(2, 1, k).then_inc(mix_block_used, 1)
                    pe.wait_ge(mix_biased, TILES - 1)
                pe.wait_ge(sems["tokens_lo"], 1)
                for k in range(KB):
                    pe.wait_ge(sems["weights_lo"], k + 1)
                    last = product_block(0, 0, k)
                last.then_inc(sems["half_done"], 2)
                if not is_high:
                    pe.wait_ge(mix_biased, TILES)
                linear_tile(1, 1)
                with pe.Fori(1, TILES // 2 - 1) as i:
                    for p in range(2):
                        pe.wait_ge(sems["summed"], 4 * i + 2 * p - 2)
                        linear_tile(2 * i + p, p)
                pe.wait_ge(sems["summed"], 2 * TILES - 6)
                linear_tile(TILES - 2, 0)
                if not is_high:
                    pe.wait_ge(any_made, 1)
                    nc.tensor.matmul(acc[0:1, 4, 0:1], any_high, one_col, start=True,
                                     stop=True).then_inc(flag_counted, 1)
                pe.wait_ge(sems["summed"], 2 * TILES - 4)
                linear_tile(TILES - 1, 1)

            linear(low, False)
            pe.wait_ge(flag_made, 1)
            wanted = nc.tensor.value_load(flag[0:1, 0:1], min_val=0, max_val=1)
            with nc.tensor.If(wanted > 0):
                linear(hi8, True)

        @block.scalar
        def _(act):
            act.wait_ge(consts_made, 2)
            nc.scalar.activation(stats[:, 0, 0:1], half_power, ACT.Gelu)
            def load_q(b):
                act.dma_start(q_low[:, :, :], qbits[bass.ds(b * P, P), 0:LOW_BITS, :]).then_inc(q_loaded, 16)

            def split_mix_rows(g):
                act.wait_ge(banks_free, 8 + 8 * (g // 4) + 4 + g % 4 + 1)
                nc.scalar.activation(mat_hi[:, g, :], weights[:, MASK_SLOT + g % 4, :],
                                     ACT.Copy).then_inc(mix_hi_made, 1)

            for c in range(CHUNKS):
                s, d = c % 2, c % KB
                act.wait_ge(w1_loaded[s], 16 * (c // 2 + 1))
                if c >= 2:
                    chunk_done(act, c - 2)
                nc.scalar.activation(split_hi[:, s, 0:HALF], w1_stage[:, s, :], ACT.Copy).then_inc(w1_hi_made, 1)
                if c == 0:
                    for t in range(2):
                        half = slice(t * HALF, (t + 1) * HALF)
                        act.wait_ge(w2_first_loaded[t], 16)
                        nc.scalar.activation(w2_hi[:, 0, half], stage[:, 0, half], ACT.Copy).then_inc(w2_hi_made, 1)
                    load_q(0)
                elif c < KB:
                    act.wait_ge(w2_loaded[s], 16 * ((d + 1) // 2))
                    nc.scalar.activation(w2_hi[:, d, :], stage[:, STAGE_OF[s], :], ACT.Copy).then_inc(w2_hi_made, 1)
                if c == KB + 1:
                    for g in range(4):
                        split_mix_rows(g)
                steps = sum(n for at, n in EARLY.items() if at < c - 2)
                for b in blocks_started(steps, steps + EARLY.get(c - 2, 0)):
                    act.wait_ge(planes_made, b + 1)
                    load_q(b + 1)

            def split_x_cols(j, p):
                act.wait_ge(x_cols_loaded, 16 * j + 16)
                nc.scalar.activation(split_hi[:, p, :], stage[:, 0, :], ACT.Copy).then_inc(x_hi_made, 1)

            for p in range(2):
                chunk_done(act, CHUNKS - 2 + p)
                split_x_cols(p, p)
                split_mix_rows(4 + 2 * p)
                split_mix_rows(5 + 2 * p)
            steps = sum(n for at, n in EARLY.items() if at < CHUNKS - 2)
            for b in blocks_started(steps, EARLY_ALL):
                act.wait_ge(planes_made, b + 1)
                load_q(b + 1)

            def gelu(j):
                act.wait_ge(mix_biased, j + 1)
                nc.scalar.activation(x1[:, j, :], x1[:, j, :], ACT.Gelu).then_inc(gelu_done, 1)

            def squares1(j, p, more_rows):
                col = slice(p, p + 1)
                if more_rows:
                    act.wait_ge(residual_done, j + 1)
                    act.dma_start(stage[:, 2, :], x_rows[bass.ds((j + 1) * P, P), :]).then_inc(x_rows_loaded, 16)
                act.wait_ge(mean1, j + 1)
                if j:
                    act.wait_ge(energy_ready, j)
                nc.scalar.activation(junk[:, :], x1[:, j, :], ACT.Square, bias=neg_mean[:, col],
                                     accum_out=sqsum[:, col]).then_inc(squared1, 1)

            def scale1(j, p):
                col = slice(p, p + 1)
                act.wait_ge(shift1, j + 1)
                nc.scalar.activation(x1[:, j, :], x1[:, j, :], ACT.Identity, bias=shift[:, col],
                                     scale=rstd[:, col]).then_inc(x1_ready, 1)
                act.wait_ge(x1_ready, j + 1)
                nc.scalar.activation(junk[:, :], x1[:, j, :], ACT.Square,
                                     accum_out=energy[:, bass.ds(j, 1)]).then_inc(energy_ready, 1)

            for j in range(TILES - 2):
                act.wait_ge(mixed, j + 1)
                split_x_cols(j + 2, j % 2)
                gelu(j)
                if j:
                    scale1(j - 1, (j - 1) % 2)
                squares1(j, j % 2, True)
                for b in blocks_started(steps_by(j - 1), steps_by(j)):
                    if b + 1 < KB:
                        act.wait_ge(planes_made, b + 1)
                        load_q(b + 1)

            def linear(sems, is_high):
                def split_tokens(p, turn):
                    act.wait_ge(sems["tokens_turned"][p], 16 * MOVES * turn)
                    nc.scalar.activation(turned(split_hi[:, p, :]), features_by_token(moved[:, p, :]),
                                         ACT.Copy).then_inc(sems["tokens_hi"], 1)

                def split_weights(k):
                    act.wait_ge(sems["rows_moved"], 16 * MOVES * KB)
                    if not is_high:
                        act.wait_ge(mix_block_used, k + 1)
                    nc.scalar.activation(by_group(mat_hi[:, k, :]), turned_weights(k),
                                         ACT.Copy).then_inc(sems["weights_hi"], 1)

                if not is_high:
                    scale1(TILES - 3, 1)
                    act.wait_ge(mixed, TILES - 1)
                    gelu(TILES - 2)
                split_weights(0)
                split_weights(1)
                split_tokens(0, 1)
                split_weights(2)
                if not is_high:
                    squares1(TILES - 2, 0, True)
                for k in range(3, KB):
                    split_weights(k)
                split_tokens(1, 1)
                if not is_high:
                    gelu(TILES - 1)
                    scale1(TILES - 2, 0)
                act.wait_ge(sems["blocks_turned"], 3)
                act.wait_ge(sems["tokens_lo"], 1)
                move_tokens(act, sems, 0)
                if not is_high:
                    squares1(TILES - 1, 1, False)
                    scale1(TILES - 1, 1)

                def tile(i, p, more):
                    j = 2 * i + p
                    act.wait_ge(sems["half_done"], 2 * j + 2)
                    split_tokens(p, i + 2)
                    if more:
                        act.wait_ge(sems["blocks_turned"], j + 4)
                        act.wait_ge(sems["tokens_lo"], j + 2)
                        move_tokens(act, sems, 1 - p)

                with act.Fori(0, TILES // 2 - 2) as i:
                    for p in range(2):
                        tile(i, p, True)
                tile(TILES // 2 - 2, 0, True)
                tile(TILES // 2 - 2, 1, False)

            linear(low, False)
            act.wait_ge(flag_made, 1)
            wanted = nc.scalar.value_load(flag[0:1, 0:1], min_val=0, max_val=1)
            with nc.scalar.If(wanted > 0):
                linear(hi8, True)

        @block.vector
        def _(dve):
            def make_planes(b, base):
                dve.wait_ge(q_loaded, 16 * b + 16)
                if b:
                    dve.wait_ge(decoded, base)
                q16 = q_low[:, :, :].bitcast(u16)
                for s in range(16):
                    last = nc.vector.tensor_scalar(planes[:, :, s * W16:(s + 1) * W16], q16, 1 << s, None,
                                                   ALU.bitwise_and)
                last.then_inc(planes_made, 1)
                dve.wait_ge(planes_made, b + 1)
                nc.vector.tensor_scalar(bit0_mask, plane0, 0.0, -1.0, ALU.is_gt, ALU.mult).then_inc(decoded, 1)

            def quarter(b, count, q, dest):
                if q in (0, 2):
                    dve.wait_ge(decoded, count)
                for n, to in ((0, dest), (1, leaf)):
                    if n == 1 and q in (1, 3):
                        dve.wait_ge(decoded, count)
                    leaf_no = 2 * q + n
                    last = nc.vector.tensor_scalar(to.bitcast(u32), bit0_mask.bitcast(u32),
                                                   lut_flip[:, b, leaf_no:leaf_no + 1],
                                                   lut[:, b, 2 * leaf_no:2 * leaf_no + 1].bitcast(u32),
                                                   ALU.bitwise_and, ALU.bitwise_xor)
                last.then_inc(decoded, 1)
                dve.wait_ge(decoded, count + 1)
                nc.vector.copy_predicated(dest, planes[:, 1, :], leaf).then_inc(decoded, 1)

            def merge(count, plane, dest, other):
                dve.wait_ge(decoded, count)
                nc.vector.copy_predicated(dest, planes[:, plane, :], other).then_inc(decoded, 1)

            def decode_step(n):
                b, step = divmod(n, STEPS)
                base, dest = DECODE_COUNT * b, weights[:, b, :]
                tmp, tmp2 = ((weights[:, b + 1, :], weights[:, b + 2, :]) if n < EARLY_ALL
                             else (x1[:, TILES - 2, :], x1[:, TILES - 1, :]))
                if b and step == (2 if b == 1 else 5):
                    dve.wait_ge(low["rows_moved"], 16 * MOVES * b)
                if step == 0:
                    make_planes(b, base)
                elif step == 1:
                    quarter(b, base + 1, 0, dest)
                elif step == 2:
                    quarter(b, base + 3, 1, tmp)
                elif step == 3:
                    merge(base + 5, 2, dest, tmp)
                elif step == 4:
                    quarter(b, base + 6, 2, tmp)
                elif step == 5:
                    quarter(b, base + 8, 3, tmp2)
                elif step == 6:
                    merge(base + 10, 2, tmp, tmp2)
                elif step == 7:
                    merge(base + 11, 3, dest, tmp)
                else:
                    dve.wait_ge(decoded, base + DECODE_COUNT)
                    nc.vector.transpose(turn_slot(b), weight_blocks(dest)).then_inc(low["rows_turned"], 1)

            def mask_mix_banks(r, t, sb_):
                dve.wait_ge(mask_loaded[sb_], 16 * (r + 1))
                dve.wait_ge(mix_bank_done, 8 * r + 4 * t + sb_ + 1)
                rows = weights[:, MASK_SLOT + sb_, t * HALF:(t + 1) * HALF]
                nc.vector.tensor_tensor(rows, acc[:, 4 * t + sb_, :], rows, ALU.mult).then_inc(banks_free, 1)

            def mix_lo(g):
                dve.wait_ge(mix_hi_made, g + 1)
                nc.vector.tensor_tensor(mat_lo[:, g, :], weights[:, MASK_SLOT + g % 4, :],
                                        mat_hi[:, g, :].bitcast(f32), ALU.subtract).then_inc(mix_lo_made, 1)

            def w2_lo_of(d, slot, cols):
                nc.vector.tensor_tensor(w2_lo[:, d, cols], stage[:, slot, cols], w2_hi[:, d, cols].bitcast(f32),
                                        ALU.subtract).then_inc(w2_lo_made, 1)

            step = 0
            for c in range(CHUNKS):
                s, d = c % 2, c % KB
                dve.wait_ge(w1_hi_made, c + 1)
                nc.vector.tensor_tensor(split_lo[:, s, 0:HALF], w1_stage[:, s, :],
                                        split_hi[:, s, 0:HALF].bitcast(f32), ALU.subtract).then_inc(w1_lo_made, 1)
                if c == 0:
                    for t in range(2):
                        dve.wait_ge(w2_hi_made, t + 1)
                        w2_lo_of(0, 0, slice(t * HALF, (t + 1) * HALF))
                elif c < KB:
                    dve.wait_ge(w2_hi_made, d + 2)
                    w2_lo_of(d, STAGE_OF[s], slice(0, D))
                if c == 1:
                    dve.wait_ge(lut_loaded, 16)
                    pairs = lut[:, :, :].bitcast(u32).rearrange("p b (j t) -> p b j t", t=2)
                    nc.vector.tensor_tensor(lut_flip[:, :, :], pairs[:, :, :, 0], pairs[:, :, :, 1],
                                            ALU.bitwise_xor).then_inc(flips_made, 1)
                    dve.wait_ge(flips_made, 1)
                if c == KB:
                    for t in range(2):
                        for sb_ in range(4):
                            mask_mix_banks(0, t, sb_)
                for _ in range(EARLY.get(c, 0)):
                    decode_step(step)
                    step += 1
            for sb_ in range(4):
                mask_mix_banks(1, 0, sb_)
            for sb_ in range(4):
                mask_mix_banks(1, 1, sb_)
                if sb_ >= 1:
                    mix_lo(3 + sb_)
            mix_lo(7)

            def bias_mix(j, p):
                if j < TILES - 1:
                    dve.wait_ge(mixed, j + 1)
                else:
                    dve.wait_ge(mix_block_used, KB)
                dve.wait_ge(b2_loaded, 16)
                nc.vector.tensor_tensor(x1[:, j, :], banks(2 * p), row_bc[:, :], ALU.add).then_inc(mix_biased, 1)

            def residual(j, p):
                dve.wait_ge(gelu_done, j + 1)
                dve.wait_ge(x_rows_loaded, 16 * j + 16)
                nc.vector.scalar_tensor_tensor(x1[:, j, :], x1[:, j, :], 1.0, stage[:, 2, :], ALU.mult, ALU.add,
                                               accum_out=zsum[:, p:p + 1]).then_inc(residual_done, 1)

            for j in range(TILES - 2):
                bias_mix(j, j % 2)
                for n in range(steps_by(j - 1), steps_by(j)):
                    if n == steps_by(j - 1) + 1:
                        residual(j, j % 2)
                    decode_step(n)

            def linear(sems, is_high):
                def turn_blocks(j, p):
                    if not is_high:
                        dve.wait_ge(x1_ready, j + 1)
                    if j >= 2:
                        dve.wait_ge(sems["tokens_turned"][p], 16 * MOVES * (j // 2))
                    nc.vector.transpose(stage[:, p, :], token_blocks(x1[:, j, :])).then_inc(
                        sems["blocks_turned"], 1)

                def tokens_lo(j, p):
                    dve.wait_ge(sems["tokens_hi"], j + 1)
                    nc.vector.tensor_tensor(turned(split_lo[:, p, :]), features_by_token(moved[:, p, :]),
                                            turned(split_hi[:, p, :].bitcast(f32)),
                                            ALU.subtract).then_inc(sems["tokens_lo"], 1)

                def weights_lo(k):
                    dve.wait_ge(sems["weights_hi"], k + 1)
                    nc.vector.tensor_tensor(by_group(mat_lo[:, k, :]), turned_weights(k),
                                            by_group(mat_hi[:, k, :].bitcast(f32)),
                                            ALU.subtract).then_inc(sems["weights_lo"], 1)

                def add_bias(j, s):
                    nc.vector.tensor_tensor(weights[:, s, :], x1[:, j, :], row_bc[:, :],
                                            ALU.add).then_inc(sems["biased"], 1)

                if is_high:
                    for b in range(KB):
                        if b:
                            dve.wait_ge(sems["rows_moved"], 16 * MOVES * b)
                        nc.vector.transpose(stage[:, 0, :], weight_blocks(weights[:, b, :])).then_inc(
                            sems["rows_turned"], 1)
                    dve.wait_ge(sems["rows_moved"], 16 * MOVES * KB)
                else:
                    dve.wait_ge(decoded, DECODED_ALL)
                    dve.wait_ge(x_lo_made, TILES)
                turn_blocks(0, 0)
                if not is_high:
                    bias_mix(TILES - 2, 0)
                turn_blocks(1, 1)
                if not is_high:
                    residual(TILES - 2, 0)
                weights_lo(0)
                weights_lo(1)
                tokens_lo(0, 0)
                for k in range(2, KB - 2):
                    weights_lo(k)
                if not is_high:
                    dve.wait_ge(low["rows_moved"], 16 * MOVES * KB)
                    bias_mix(TILES - 1, 1)
                for k in range(KB - 2, KB):
                    weights_lo(k)
                tokens_lo(1, 1)
                turn_blocks(2, 0)
                if not is_high:
                    residual(TILES - 1, 1)
                dve.wait_ge(sems["weights_lo"], KB)
                dve.wait_ge(bias_loaded, 16)
                if not is_high:
                    dve.wait_ge(x1_ready, 2)
                add_bias(0, 0)
                add_bias(1, 1)

                def tile(j):
                    p, s = j % 2, j % RING
                    for t in range(2):
                        half = slice(t * HALF, (t + 1) * HALF)
                        dve.wait_ge(sems["half_done"], 2 * j + t + 1)
                        if t == 0:
                            dve.wait_ge(sems["biased"], j + 1)
                        nc.vector.tensor_tensor(weights[:, s, half], acc[:, 2 * p + t, :], weights[:, s, half],
                                                ALU.add).then_inc(sems["summed"], 1)
                        if t == 0 and j + 3 < TILES:
                            turn_blocks(j + 3, 1 - p)
                        dve.wait_ge(sems["summed"], 2 * j + t + 1)
                        nc.vector.bn_stats(halves[:, t, :], weights[:, s, half]).then_inc(sems["half_stats"], 1)
                    dve.wait_ge(sems["half_stats"], 2 * j + 2)
                    nc.vector.bn_aggr(moments[:, p, :], halves[:, :, :].rearrange("p a b -> p (a b)")).then_inc(
                        sems["tile_stats"], 1)
                    if j + 2 < TILES:
                        tokens_lo(j + 2, p)
                        if j >= 2:
                            dve.wait_ge(sems["stored"][(j + 2) % RING], 32 * ((j + 2) // RING))
                        add_bias(j + 2, (j + 2) % RING)
                    dve.wait_ge(sems["rstd"], j + 1)
                    for t in range(2):
                        rows = weights[:, s, t * HALF:(t + 1) * HALF]
                        nc.vector.tensor_scalar(rows, rows, moments[:, p, 0:1], rstd[:, p:p + 1],
                                                ALU.subtract, ALU.mult).then_inc(sems["normed"], 1)
                    if is_high:
                        rows = weights[:, s, :].bitcast(i32)
                        kept = stage[:, 2, :].bitcast(i32)
                        dve.wait_ge(sems["normed"], 2 * j + 2)
                        dve.wait_ge(sems["low_rows_loaded"], 16 * j + 16)
                        nc.vector.tensor_tensor(rows, rows, kept, ALU.bitwise_xor).then_inc(sems["compared"], 1)
                        dve.wait_ge(sems["compared"], j + 1)
                        nc.vector.scalar_tensor_tensor(kept, rows, high_bits[:, j:j + 1], kept,
                                                       ALU.bitwise_and, ALU.bitwise_xor).then_inc(sems["blended"], 1)

                for j in range(TILES):
                    tile(j)
                    if j == TILES - 3 and not is_high:
                        decide()

            def decide():
                dve.wait_ge(high_made, 1)
                nc.vector.tensor_scalar(high_bits[:, :], high, -1.0, None, ALU.mult)
                nc.vector.reduce_max(any_high, high, mybir.AxisListType.X).then_inc(any_made, 1)
                dve.wait_ge(flag_counted, 1)
                nc.vector.tensor_scalar(flag[0:1, 0:1], acc[0:1, 4, 0:1], 0.0, None, ALU.is_gt).then_inc(flag_made, 1)

            linear(low, False)
            dve.wait_ge(flag_made, 1)
            wanted = nc.vector.value_load(flag[0:1, 0:1], min_val=0, max_val=1)
            with nc.vector.If(wanted > 0):
                for s in range(RING):
                    dve.wait_ge(low["stored"][s], 32 * (TILES // RING))
                q_high = stage[:, 2, 0:HIGH_BITS * WORDS].bitcast(u16).rearrange("p (n w) -> p n w", n=HIGH_BITS)
                table = stage[:, 2, 256:512]
                code, bits, hit = stage[:, 1, :], planes[:, 1, :], stage[:, 0, :].bitcast(i32)
                with dve.Fori(0, KB) as b:
                    base = HIGH_STEPS * b
                    dve.wait_ge(high_bits_loaded, 32 * b + 32)
                    row = weights[:, b, :].bitcast(i32)
                    nc.vector.tensor_scalar(row, row, 0, None, ALU.bitwise_and).then_inc(high_step, 1)
                    dve.wait_ge(high_step, base + 1)
                    nc.vector.tensor_scalar(code.bitcast(i32), code.bitcast(i32), 0, None,
                                            ALU.bitwise_and).then_inc(high_step, 1)
                    for n in range(HIGH_BITS):
                        dve.wait_ge(high_step, base + 2 * n + 2)
                        for s in range(16):
                            last = nc.vector.tensor_scalar(bits[:, s * W16:(s + 1) * W16],
                                                           q_high[:, HIGH_BITS - 1 - n, :], s, 1,
                                                           ALU.logical_shift_right, ALU.bitwise_and)
                        last.then_inc(high_step, 1)
                        dve.wait_ge(high_step, base + 2 * n + 3)
                        nc.vector.scalar_tensor_tensor(code, code, 2.0, bits, ALU.mult,
                                                       ALU.add).then_inc(high_step, 1)
                    with dve.Fori(0, 2 ** HIGH_BITS) as k:
                        dve.wait_ge(high_step, base + 2 + 2 * HIGH_BITS + 2 * k)
                        nc.vector.tensor_scalar(hit, code, 0.0, -1.0, ALU.is_equal, ALU.mult).then_inc(high_step, 1)
                        dve.wait_ge(high_step, base + 3 + 2 * HIGH_BITS + 2 * k)
                        nc.vector.scalar_tensor_tensor(row, hit, table[:, bass.ds(k, 1)].bitcast(i32), row,
                                                       ALU.bitwise_and, ALU.bitwise_or)
                        nc.vector.tensor_scalar(code, code, -1.0, None, ALU.add).then_inc(high_step, 1)
                dve.wait_ge(high_step, HIGH_STEPS * KB)
                linear(hi8, True)

        @block.gpsimd
        def _(pool):
            nc.gpsimd.memset(junk[:, 0:HALF], 1.0).then_inc(warm_made, 1)
            nc.gpsimd.memset(half_powers, 0.5).then_inc(consts_made, 1)
            nc.gpsimd.memset(half_power, 0.5).then_inc(consts_made, 1)
            nc.gpsimd.memset(minus_half_power, -0.5).then_inc(consts_made, 1)
            nc.gpsimd.memset(one_col, 1.0).then_inc(consts_made, 1)
            nc.gpsimd.memset(inv_d, 1.0 / D).then_inc(consts_made, 1)
            nc.gpsimd.memset(neg_inv_d, -1.0 / D).then_inc(consts_made, 1)
            nc.gpsimd.memset(eps_col, EPS).then_inc(consts_made, 1)
            nc.gpsimd.memset(zero_col, 0.0).then_inc(banks_free, 8)
            pool.wait_ge(consts_made, 7)

            def statistics1(j, p):
                col = slice(p, p + 1)
                pool.wait_ge(residual_done, j + 1)
                nc.gpsimd.tensor_tensor(neg_mean[:, col], zsum[:, col], neg_inv_d, ALU.mult).then_inc(mean1, 1)
                pool.wait_ge(squared1, j + 1)
                nc.gpsimd.tensor_tensor(var[:, col], sqsum[:, col], inv_d, ALU.mult).then_inc(var1, 1)
                pool.wait_ge(var1, 2 * j + 1)
                nc.gpsimd.tensor_tensor(var[:, col], var[:, col], eps_col, ALU.add).then_inc(var1, 1)
                pool.wait_ge(var1, 2 * j + 2)
                nc.gpsimd.tensor_tensor(rstd[:, col], var[:, col], minus_half_power, ALU.pow).then_inc(rstd1, 1)
                pool.wait_ge(rstd1, j + 1)
                nc.gpsimd.tensor_tensor(shift[:, col], neg_mean[:, col], rstd[:, col], ALU.mult).then_inc(shift1, 1)

            def x_lo(j, p):
                pool.wait_ge(x_hi_made, j + 1)
                nc.gpsimd.tensor_tensor(split_lo[:, p, :], stage[:, 0, :], split_hi[:, p, :].bitcast(f32),
                                        ALU.subtract).then_inc(x_lo_made, 1)

            for g in range(4):
                pool.wait_ge(mix_hi_made, g + 1)
                nc.gpsimd.tensor_tensor(mat_lo[:, g, :], weights[:, MASK_SLOT + g % 4, :],
                                        mat_hi[:, g, :].bitcast(f32), ALU.subtract).then_inc(mix_lo_made, 1)
            for p in range(2):
                x_lo(p, p)
            with pool.Fori(0, TILES // 2 - 1) as i:
                for p in range(2):
                    x_lo(2 * i + p + 2, p)
                    statistics1(2 * i + p, p)
            statistics1(TILES - 2, 0)
            statistics1(TILES - 1, 1)

            pool.wait_ge(energy_ready, TILES)
            nc.gpsimd.tensor_tensor(norm, energy[:, :], half_powers, ALU.pow).then_inc(norm_made, 1)
            pool.wait_ge(norm_made, 1)
            nc.gpsimd.tensor_scalar(norm, norm, LIN_SLOPE, LIN_INTER, ALU.mult, ALU.add).then_inc(norm_made, 1)
            pool.wait_ge(norm_made, 2)
            nc.gpsimd.tensor_scalar(high, norm, EST_T, None, ALU.is_gt).then_inc(high_made, 1)

            def linear(sems):
                with pool.Fori(0, TILES // 2) as i:
                    for p in range(2):
                        j, col = 2 * i + p, slice(p, p + 1)
                        pool.wait_ge(sems["tile_stats"], j + 1)
                        nc.gpsimd.tensor_tensor(var[:, col], moments[:, p, 1:2], eps_col,
                                                ALU.add).then_inc(sems["variance"], 1)
                        pool.wait_ge(sems["variance"], j + 1)
                        nc.gpsimd.tensor_tensor(rstd[:, col], var[:, col], minus_half_power,
                                                ALU.pow).then_inc(sems["rstd"], 1)

            linear(low)
            pool.wait_ge(flag_made, 1)
            wanted = nc.gpsimd.value_load(flag[0:1, 0:1], min_val=0, max_val=1)
            with nc.gpsimd.If(wanted > 0):
                linear(hi8)


def kernel(L0_attn_x, L0_attn_w1, L0_attn_w2, L0_attn_b2, L0_attn_sparse_mask, L0_ffn_qweight, L0_ffn_lut4,
           L0_ffn_lut8, L0_ffn_bias):
    import concourse.bacc as bacc
    from concourse.bass_utils import run_bass_kernel_spmd as run

    x = np.asarray(L0_attn_x)
    batch, seq, d = x.shape
    tokens = batch * seq
    rows = np.ascontiguousarray(x.reshape(tokens, d))
    cols = np.ascontiguousarray(rows.reshape(tokens // P, P, d // P, P).transpose(0, 3, 2, 1)).reshape(
        tokens // P, P, d)
    arrays = {
        "x_rows": rows,
        "x_cols": cols,
        "w1": np.ascontiguousarray(L0_attn_w1),
        "w2_cols": np.ascontiguousarray(np.asarray(L0_attn_w2).T),
        "b2": np.ascontiguousarray(L0_attn_b2).reshape(1, d),
        "mask": np.ascontiguousarray(L0_attn_sparse_mask),
        "qbits": np.ascontiguousarray(np.asarray(L0_ffn_qweight).transpose(1, 0, 2)),
        "lut4": np.ascontiguousarray(np.asarray(L0_ffn_lut4).reshape(d // P, P, -1).transpose(1, 0, 2)),
        "lut8": np.ascontiguousarray(L0_ffn_lut8),
        "bias": np.ascontiguousarray(L0_ffn_bias).reshape(1, d),
    }
    nc = bacc.Bacc("TRN2", target_bir_lowering=False, num_devices=1)
    args = [nc.dram_tensor(f"in_{name}", a.shape, mybir.dt.from_np(a.dtype), kind="ExternalInput").ap()
            for name, a in arrays.items()]
    out = nc.dram_tensor("out_rows", (tokens, d), mybir.dt.float32, kind="ExternalOutput").ap()
    post_ln_block(nc, *args, out)
    result = run(nc, [{f"in_{name}": a for name, a in arrays.items()}], core_ids=[0])
    return result.results[0]["out_rows"].reshape(batch, seq, d)
```
